# Optimizing a Trainium2 kernel written in Bass

```python
import numpy as np
import jax
import jax.numpy as jnp

def _softmax(x, axis=-1):
    return jax.nn.softmax(x, axis=axis)

def _gelu(x):
    return jax.nn.gelu(x, approximate=True)

def _silu(x):
    return jax.nn.silu(x)

def _sigmoid(x):
    return jax.nn.sigmoid(x)

def _layernorm(x, axis=-1, eps=1e-05):
    m = jnp.mean(x, axis=axis, keepdims=True)
    v = jnp.var(x, axis=axis, keepdims=True)
    return (x - m) / jnp.sqrt(v + eps)

def _scatter_add(tgt, idx, src, axis=0):
    return tgt.at[idx].add(src)

def _segment_sum(src, seg, n):
    return jax.ops.segment_sum(src, seg, n)
kernel_name = 'mk_early_fusion_d1_tok_img256_r4_998bc0'

def setup_inputs(seed: int=0):
    np.random.seed(seed)
    _w = jnp.asarray

    def _rec_inputs():
        import jax
        import jax.numpy as jnp
        _rk = jax.random.key(seed)
        x = 7.57192e-06 + 1.00007 * jax.random.normal(jax.random.fold_in(_rk, 1), (64, 3, 224, 224), jnp.float32)
        txt = 0.00191194 + 0.0219993 * jax.random.normal(jax.random.fold_in(_rk, 2), (64, 77, 64), jnp.float32)
        return (x, txt)
    x, txt = _rec_inputs()

    def _L0_tok_setup():
        import jax, jax.numpy as jnp
        import numpy as np
        import math
        GRID = 28
        NUM_PATCHES = GRID * GRID
        PATCH = 8
        IN_CH = 3
        HIDDEN = 64
        BATCH = 64

        def build_grid_edges():
            edges = []
            for i in range(GRID):
                for j in range(GRID):
                    cur = i * GRID + j
                    if j < GRID - 1:
                        edges.append([cur, cur + 1])
                    if i < GRID - 1:
                        edges.append([cur, cur + GRID])
            e = np.asarray(edges, dtype=np.int32).T
            e = np.concatenate([e, e[::-1]], axis=1)
            return jnp.asarray(e)

        def sin_positional_encoding(n, d):
            pos = jnp.arange(n, dtype=jnp.float32)[:, None]
            div = jnp.exp(jnp.arange(0, d, 2, dtype=jnp.float32) * (-math.log(10000.0) / d))
            pe = jnp.zeros((n, d), dtype=jnp.float32)
            pe = pe.at[:, 0::2].set(jnp.sin(pos * div))
            pe = pe.at[:, 1::2].set(jnp.cos(pos * div))
            return pe
        key = jax.random.key(seed)
        ks = jax.random.split(key, 8)
        s = 0.02
        return {'x': jax.random.normal(ks[0], (BATCH, IN_CH, 224, 224), dtype=jnp.float32), 'W_embed': jax.random.normal(ks[1], (IN_CH * PATCH * PATCH, HIDDEN), dtype=jnp.float32) * s, 'b_embed': jax.random.normal(ks[2], (HIDDEN,), dtype=jnp.float32) * s, 'W_gcn': jax.random.normal(ks[3], (3, HIDDEN, HIDDEN), dtype=jnp.float32) * s, 'b_gcn': jax.random.normal(ks[4], (3, HIDDEN), dtype=jnp.float32) * s, 'W_out': jax.random.normal(ks[5], (HIDDEN, 64), dtype=jnp.float32) * s, 'b_out': jax.random.normal(ks[6], (64,), dtype=jnp.float32) * s, 'edge_index': build_grid_edges()}
    _L0_tok_all = _L0_tok_setup()
    _L0_tok_in = {k: v for k, v in _L0_tok_all.items() if k in ('W_embed', 'b_embed', 'W_gcn', 'b_gcn', 'W_out', 'b_out', 'edge_index')}
    del _L0_tok_all

    def _L0_attn_setup():
        import jax, jax.numpy as jnp
        import numpy as np
        DIM = 64
        HEADS = 4
        HEAD_DIM = DIM // HEADS
        SCALE = HEAD_DIM ** (-0.5)
        key = jax.random.key(seed)
        ks = jax.random.split(key, 9)
        B, N, C = (2, 1024, DIM)
        x = jax.random.normal(ks[0], (B, N, C), dtype=jnp.float32)
        lim = np.sqrt(6.0 / (C + C)).astype(np.float32)

        def w(k):
            return jax.random.uniform(k, (C, C), dtype=jnp.float32, minval=-lim, maxval=lim)
        return {'x': x, 'Wq': w(ks[1]), 'bq': jnp.zeros((C,), jnp.float32), 'Wk': w(ks[2]), 'bk': jnp.zeros((C,), jnp.float32), 'Wv': w(ks[3]), 'bv': jnp.zeros((C,), jnp.float32), 'Wo': w(ks[4]), 'bo': jnp.zeros((C,), jnp.float32)}
    _L0_attn_all = _L0_attn_setup()
    _L0_attn_in = {k: v for k, v in _L0_attn_all.items() if k in ('Wq', 'bq', 'Wk', 'bk', 'Wv', 'bv', 'Wo', 'bo')}
    del _L0_attn_all

    def _L0_ffn_setup():
        import jax, jax.numpy as jnp
        import numpy as np
        B, A = (1024, 8)
        IN, OUT = (64, 64)
        SH1, SH2 = (64, 128)
        EH1, EH2 = (128, 64)
        E, TOPK = (4, 2)

        def _shared_mlp(x, W1, b1, W2, b2, W3, b3):
            h = jax.nn.relu(x @ W1 + b1)
            h = jax.nn.relu(h @ W2 + b2)
            return h @ W3 + b3

        def _experts_mlp(x, eW1, eb1, eW2, eb2, eW3, eb3):
            h = jax.nn.relu(jnp.einsum('baf,efh->ebah', x, eW1) + eb1[:, None, None, :])
            h = jax.nn.relu(jnp.einsum('ebah,ehg->ebag', h, eW2) + eb2[:, None, None, :])
            o = jnp.einsum('ebag,ego->ebao', h, eW3) + eb3[:, None, None, :]
            return jnp.moveaxis(o, 0, -1)
        key = jax.random.key(seed)
        ks = jax.random.split(key, 16)
        s = 0.05
        return {'x': jax.random.normal(ks[0], (B, A, IN), jnp.float32), 'sW1': jax.random.normal(ks[1], (IN, SH1), jnp.float32) * s, 'sb1': jnp.zeros((SH1,), jnp.float32), 'sW2': jax.random.normal(ks[2], (SH1, SH2), jnp.float32) * s, 'sb2': jnp.zeros((SH2,), jnp.float32), 'sW3': jax.random.normal(ks[3], (SH2, OUT), jnp.float32) * s, 'sb3': jnp.zeros((OUT,), jnp.float32), 'eW1': jax.random.normal(ks[4], (E, IN, EH1), jnp.float32) * s, 'eb1': jnp.zeros((E, EH1), jnp.float32), 'eW2': jax.random.normal(ks[5], (E, EH1, EH2), jnp.float32) * s, 'eb2': jnp.zeros((E, EH2), jnp.float32), 'eW3': jax.random.normal(ks[6], (E, EH2, OUT), jnp.float32) * s, 'eb3': jnp.zeros((E, OUT), jnp.float32), 'gW': jax.random.normal(ks[7], (IN, E), jnp.float32) * s, 'gb': jnp.zeros((E,), jnp.float32)}
    _L0_ffn_all = _L0_ffn_setup()
    _L0_ffn_in = {k: v for k, v in _L0_ffn_all.items() if k in ('sW1', 'sb1', 'sW2', 'sb2', 'sW3', 'sb3', 'eW1', 'eb1', 'eW2', 'eb2', 'eW3', 'eb3', 'gW', 'gb')}
    del _L0_ffn_all
    return {'x': x, 'txt': txt, 'L0_tok_W_embed': _L0_tok_in['W_embed'], 'L0_tok_b_embed': _L0_tok_in['b_embed'], 'L0_tok_W_gcn': _L0_tok_in['W_gcn'], 'L0_tok_b_gcn': _L0_tok_in['b_gcn'], 'L0_tok_W_out': _L0_tok_in['W_out'], 'L0_tok_b_out': _L0_tok_in['b_out'], 'L0_tok_edge_index': _L0_tok_in['edge_index'], 'L0_attn_Wq': _L0_attn_in['Wq'], 'L0_attn_bq': _L0_attn_in['bq'], 'L0_attn_Wk': _L0_attn_in['Wk'], 'L0_attn_bk': _L0_attn_in['bk'], 'L0_attn_Wv': _L0_attn_in['Wv'], 'L0_attn_bv': _L0_attn_in['bv'], 'L0_attn_Wo': _L0_attn_in['Wo'], 'L0_attn_bo': _L0_attn_in['bo'], 'L0_ffn_sW1': _L0_ffn_in['sW1'], 'L0_ffn_sb1': _L0_ffn_in['sb1'], 'L0_ffn_sW2': _L0_ffn_in['sW2'], 'L0_ffn_sb2': _L0_ffn_in['sb2'], 'L0_ffn_sW3': _L0_ffn_in['sW3'], 'L0_ffn_sb3': _L0_ffn_in['sb3'], 'L0_ffn_eW1': _L0_ffn_in['eW1'], 'L0_ffn_eb1': _L0_ffn_in['eb1'], 'L0_ffn_eW2': _L0_ffn_in['eW2'], 'L0_ffn_eb2': _L0_ffn_in['eb2'], 'L0_ffn_eW3': _L0_ffn_in['eW3'], 'L0_ffn_eb3': _L0_ffn_in['eb3'], 'L0_ffn_gW': _L0_ffn_in['gW'], 'L0_ffn_gb': _L0_ffn_in['gb']}

def reference(x, txt, L0_tok_W_embed, L0_tok_b_embed, L0_tok_W_gcn, L0_tok_b_gcn, L0_tok_W_out, L0_tok_b_out, L0_tok_edge_index, L0_attn_Wq, L0_attn_bq, L0_attn_Wk, L0_attn_bk, L0_attn_Wv, L0_attn_bv, L0_attn_Wo, L0_attn_bo, L0_ffn_sW1, L0_ffn_sb1, L0_ffn_sW2, L0_ffn_sb2, L0_ffn_sW3, L0_ffn_sb3, L0_ffn_eW1, L0_ffn_eb1, L0_ffn_eW2, L0_ffn_eb2, L0_ffn_eW3, L0_ffn_eb3, L0_ffn_gW, L0_ffn_gb):
    import jax
    import jax.numpy as jnp

    def _L0_tok_ref(x, W_embed, b_embed, W_gcn, b_gcn, W_out, b_out, edge_index):
        import jax, jax.numpy as jnp
        import numpy as np
        import math
        GRID = 28
        NUM_PATCHES = GRID * GRID
        PATCH = 8
        IN_CH = 3
        HIDDEN = 64
        BATCH = 64

        def build_grid_edges():
            edges = []
            for i in range(GRID):
                for j in range(GRID):
                    cur = i * GRID + j
                    if j < GRID - 1:
                        edges.append([cur, cur + 1])
                    if i < GRID - 1:
                        edges.append([cur, cur + GRID])
            e = np.asarray(edges, dtype=np.int32).T
            e = np.concatenate([e, e[::-1]], axis=1)
            return jnp.asarray(e)

        def sin_positional_encoding(n, d):
            pos = jnp.arange(n, dtype=jnp.float32)[:, None]
            div = jnp.exp(jnp.arange(0, d, 2, dtype=jnp.float32) * (-math.log(10000.0) / d))
            pe = jnp.zeros((n, d), dtype=jnp.float32)
            pe = pe.at[:, 0::2].set(jnp.sin(pos * div))
            pe = pe.at[:, 1::2].set(jnp.cos(pos * div))
            return pe
        B = x.shape[0]
        N = NUM_PATCHES
        p = x.reshape(B, IN_CH, GRID, PATCH, GRID, PATCH)
        p = p.transpose(0, 2, 4, 1, 3, 5).reshape(B, N, IN_CH * PATCH * PATCH)
        h = p @ W_embed + b_embed + sin_positional_encoding(N, HIDDEN)[None]
        src, dst = (edge_index[0], edge_index[1])
        deg = jnp.zeros((N,), dtype=h.dtype).at[dst].add(1.0) + 1.0
        dinv = deg ** (-0.5)
        enorm = (dinv[src] * dinv[dst])[None, :, None]
        snorm = (1.0 / deg)[None, :, None]
        for i in range(3):
            hw = h @ W_gcn[i]
            agg = hw * snorm
            agg = agg.at[:, dst].add(hw[:, src] * enorm)
            h = jax.nn.relu(agg + b_gcn[i])
        return h @ W_out + b_out

    def _L0_attn_ref(x, Wq, bq, Wk, bk, Wv, bv, Wo, bo):
        import jax, jax.numpy as jnp
        import numpy as np
        DIM = 64
        HEADS = 4
        HEAD_DIM = DIM // HEADS
        SCALE = HEAD_DIM ** (-0.5)
        B, N, C = x.shape
        x = jnp.clip(x, -10000.0, 10000.0)

        def heads(t):
            return t.reshape(B, N, HEADS, HEAD_DIM).transpose(0, 2, 1, 3)
        q = heads((x @ Wq.T + bq).astype(jnp.float32))
        k = heads((x @ Wk.T + bk).astype(jnp.float32))
        v = heads((x @ Wv.T + bv).astype(jnp.float32))
        attn = jnp.einsum('bhnd,bhmd->bhnm', q, k) * SCALE
        attn = jax.nn.softmax(attn, axis=-1)
        out = jnp.einsum('bhnm,bhmd->bhnd', attn, v)
        out = out.transpose(0, 2, 1, 3).reshape(B, N, C)
        out = out.astype(jnp.bfloat16).astype(jnp.float32)
        return out @ Wo.T + bo

    def _L0_ffn_ref(x, sW1, sb1, sW2, sb2, sW3, sb3, eW1, eb1, eW2, eb2, eW3, eb3, gW, gb):
        import jax, jax.numpy as jnp
        import numpy as np
        B, A = (1024, 8)
        IN, OUT = (64, 64)
        SH1, SH2 = (64, 128)
        EH1, EH2 = (128, 64)
        E, TOPK = (4, 2)

        def _shared_mlp(x, W1, b1, W2, b2, W3, b3):
            h = jax.nn.relu(x @ W1 + b1)
            h = jax.nn.relu(h @ W2 + b2)
            return h @ W3 + b3

        def _experts_mlp(x, eW1, eb1, eW2, eb2, eW3, eb3):
            h = jax.nn.relu(jnp.einsum('baf,efh->ebah', x, eW1) + eb1[:, None, None, :])
            h = jax.nn.relu(jnp.einsum('ebah,ehg->ebag', h, eW2) + eb2[:, None, None, :])
            o = jnp.einsum('ebag,ego->ebao', h, eW3) + eb3[:, None, None, :]
            return jnp.moveaxis(o, 0, -1)
        all_out = _experts_mlp(x, eW1, eb1, eW2, eb2, eW3, eb3)
        shared = _shared_mlp(x, sW1, sb1, sW2, sb2, sW3, sb3)
        gates = jax.nn.softmax(x @ gW + gb, axis=-1)
        topv, topi = jax.lax.top_k(gates, TOPK)
        topw = jax.nn.softmax(topv, axis=-1)
        sel = jnp.take_along_axis(all_out, topi[:, :, None, :], axis=-1)
        gated = jnp.sum(sel * topw[:, :, None, :], axis=-1)
        return shared + gated
    h = _L0_tok_ref(x, L0_tok_W_embed, L0_tok_b_embed, L0_tok_W_gcn, L0_tok_b_gcn, L0_tok_W_out, L0_tok_b_out, L0_tok_edge_index)
    h = jnp.concatenate([h, txt], axis=1)
    h = h + _L0_attn_ref(_layernorm(h, axis=-1), L0_attn_Wq, L0_attn_bq, L0_attn_Wk, L0_attn_bk, L0_attn_Wv, L0_attn_bv, L0_attn_Wo, L0_attn_bo)
    h = h + _L0_ffn_ref(_layernorm(h, axis=-1), L0_ffn_sW1, L0_ffn_sb1, L0_ffn_sW2, L0_ffn_sb2, L0_ffn_sW3, L0_ffn_sb3, L0_ffn_eW1, L0_ffn_eb1, L0_ffn_eW2, L0_ffn_eb2, L0_ffn_eW3, L0_ffn_eb3, L0_ffn_gW, L0_ffn_gb)
    return h

_drawn_inputs = setup_inputs


def setup_inputs(seed=0):
    import zlib

    import numpy as np

    out = dict(_drawn_inputs(seed))
    spreads = {'L0_attn_bq': (0.0, 0.45),
     'L0_attn_bk': (0.0, 2.0),
     'L0_attn_bv': (0.0, 0.1),
     'L0_attn_bo': (0.0, 0.1),
     'L0_ffn_sb1': (0.0, 0.8),
     'L0_ffn_sb2': (0.0, 0.1),
     'L0_ffn_sb3': (0.0, 0.1),
     'L0_ffn_eb1': (0.0, 0.8),
     'L0_ffn_eb2': (0.0, 0.427),
     'L0_ffn_eb3': (0.0, 0.1),
     'L0_ffn_gb': (0.0, 0.1)}
    factors = {'x': 8.0,
     'L0_tok_W_embed': 8.0,
     'L0_tok_b_embed': 8.0,
     'L0_tok_W_gcn': 4.294,
     'L0_tok_b_gcn': 2.703}
    for name, (base, spread) in spreads.items():
        noise = np.random.default_rng([zlib.crc32(name.encode()), seed]).standard_normal(out[name].shape)
        drawn = base * np.exp(spread * noise) if base else spread * noise
        out[name] = jnp.asarray(drawn.astype(out[name].dtype))
    for name, factor in factors.items():
        out[name] = (out[name] * factor).astype(out[name].dtype)
    return out
```

```python
from contextlib import ExitStack

import concourse.bass as bass
import numpy as np
from concourse import mybir

F32 = mybir.dt.float32
F32R = mybir.dt.float32r
BF16 = mybir.dt.bfloat16
I32 = mybir.dt.int32
ALU = mybir.AluOpType
ACT = mybir.ActivationFunctionType
AX = mybir.AxisListType

GRID, PATCH, CH, HID = 28, 8, 3, 64
PATCHES = GRID * GRID
TEXT = 77
TOKENS = PATCHES + TEXT
BLK = 123
NB = TOKENS // BLK
GBLK = 112
NG = PATCHES // GBLK
GHALF = PATCHES // 2
HEADS, HD = 4, 16
SCALE = HD ** -0.5
EXPERTS = 4
EPS = 1e-5
STACK_LOADS = 8 * 16
X_LOADS = 2 * CH * 16
EDGES = 2 * 2 * GRID * (GRID - 1)
ECH = 126
NEC = EDGES // ECH
SHIFT_ROW = 96
HW = 432
COLS = 2 * HW
HALVES = [(0, HW), (HW, HW)]
PIECES = [(0, 4 * BLK), (4 * BLK, 3 * BLK)]

def _columns(sizes):
    at, out = 0, {}
    for name, n in sizes:
        out[name] = (at, at + n)
        at += n
    return out, at


PLAIN, PLAIN_W = _columns([("emb", PATCH * 128), ("gcn", 3 * 128), ("out", 128), ("wo", 64),
                           ("eW2", EXPERTS * 64), ("sW2", 128), ("eW3", 2 * 64), ("sW3", 64),
                           ("b_emb", 1), ("b_gcn", 3), ("b_qk", 1), ("eb1", EXPERTS), ("sb1", 1),
                           ("eb2", 2), ("sb2", 1)])
SPLIT, SPLIT_W = _columns([("qk", 128), ("v", 64), ("eW1", EXPERTS * 128), ("sW1", 128), ("gW", EXPERTS)])
ROWS, ROWS_W = _columns([("b_out", 64), ("bv", 64), ("bo", 64), ("gb", EXPERTS), ("sb3", 64),
                         ("eb3", EXPERTS * 64)])
CONST, CONST_W = _columns([("ident", 128), ("pos", PATCHES), ("iota", PATCHES), ("before", 16)])


def graph_steps():
    out = [("embed", 0), ("embed", 1)]
    for layer in range(3):
        out += [("gw", layer, 0), ("gw", layer, 1), ("gagg", layer, 0), ("gagg", layer, 1)]
    return out + [("gw", 3, 0), ("gw", 3, 1)]


def project_steps(b):
    return [("xt", b, "a"), ("qk", b), ("v", b)]


def max_steps(b):
    return [("mx", b, qb, h, half) for qb in range(NB) for h in range(HEADS) for half in range(2)]


def max_row_steps(b):
    return [("mrow", b, 0), ("mrow", b, 1)]


def attention_steps(b):
    out = []
    for s in range(NB * HEADS):
        out.append(("s", b, s // HEADS, s % HEADS))
        if s >= 5 and (s - 5) % 4 == 0:
            out.append(("pv", b, (s - 5) // 4, 0))
        if s >= 6 and (s - 6) % 4 == 0:
            out.append(("pv", b, (s - 6) // 4, 1))
    return out + [("pv", b, NB - 1, 0), ("pv", b, NB - 1, 1)]


def finish_steps(b):
    return [("oev", b), ("ot", b, 0), ("ot", b, 1), ("obt", b), ("wo", b)]


def moe_steps(b):
    return [("xt", b, "m"), ("gate", b), ("l1", b, 0), ("l1", b, 1), ("g2", b), ("l1", b, 2), ("l1", b, 3),
            ("g3", b), ("hb", b), ("l1", b, 4), ("l2", b, 0), ("l2", b, 1), ("l2", b, 2), ("wb", b, 0),
            ("wb", b, 1), ("l3", b), ("back", b)]


COST = {"s": 2, "pv": 4, "mx": 1, "embed": 28, "gw": 4, "gagg": 12, "xt": 7, "qk": 4, "v": 7, "gate": 7, "l1": 4,
        "l2": 8, "wb": 7, "l3": 14, "ot": 4, "obt": 2, "wo": 5, "back": 3, "ln": 2, "g2": 2, "g3": 2}


def merge(main, side, share=1.0):
    total = share * sum(COST.get(st[0], 1) for st in main)
    out, done, passed = [], 0, 0
    whole = sum(COST.get(st[0], 1) for st in side)
    side_passed = 0
    for step in main:
        out.append(step)
        passed += COST.get(step[0], 1)
        while done < len(side) and side_passed * total <= passed * whole and passed * len(side) > done * total * 0:
            if side_passed * total > passed * whole:
                break
            if (side_passed + COST.get(side[done][0], 1) / 2) * total > passed * whole:
                break
            out.append(side[done])
            side_passed += COST.get(side[done][0], 1)
            done += 1
    return out + side[done:]


def round_steps(with_next):
    first = merge(attention_steps(0), max_steps(1)) + max_row_steps(1)
    att = attention_steps(1)
    fin = finish_steps(0)
    side = fin[1:] + [("ln", 0, "m")]
    if with_next:
        g = graph_steps()
        side = g[:1] + side + g[1:] + [("ln", 0, "a")]
    second = att[:2] + fin[:1] + merge(att[2:], side)
    fin, moe0, moe1 = finish_steps(1), moe_steps(0), moe_steps(1)
    if with_next:
        third = [fin[0], ("xt", 0, "a"), fin[1], fin[2], ("qk", 0), ("xt", 0, "m"), fin[3], ("v", 0), fin[4]]
        third += [("ln", 1, "m")] + moe0[1:6]
        rest = moe0[6:9] + [("ln", 1, "a")] + moe0[9:]
        rest += [("xt", 1, "m"), ("xt", 1, "a"), ("gate", 1), ("qk", 1), ("v", 1)] + moe1[2:]
        third += merge(rest, max_steps(0) + max_row_steps(0), 0.85)
    else:
        third = merge(fin + [("ln", 1, "m")], moe0) + moe1
    return [("hcopy",)] + first + second + third


def prologue_steps():
    return graph_steps() + [("ln", 0, "a")] + project_steps(0) + merge(max_steps(0), [("ln", 1, "a")] + project_steps(1)) \
        + max_row_steps(0)


FIXED = {"embed": 1, "gw": 2, "gagg": 2, "mx": 4, "mrow": 2, "ot": 2}
ROTATE = ("xt", "qk", "v", "gate", "l1", "l2", "wb", "l3", "back")


def turns(steps):
    count = {r: 0 for r in ("T0", "T1", "T2", "B6", "B7")}
    out, rot = {}, 0
    for st in steps:
        kind = st[0]
        if kind in FIXED:
            place = "B7" if st[FIXED[kind]] else "B6"
        elif kind == "s":
            place = f"T{st[3] % 2}"
        elif kind == "obt":
            place = "B6"
        elif kind == "wo":
            place = "B7"
        elif kind == "pv":
            if st[2:] != (0, 0):
                continue
            place = "T2"
        elif kind in ROTATE:
            place = f"T{rot % 3}"
            rot += 1
        else:
            continue
        count[place] += 1
        out[st] = (place, count[place])
    return out


def ordinal(steps):
    count, out = {}, {}
    for st in steps:
        count[st[0]] = count.get(st[0], 0) + 1
        out[st] = count[st[0]]
    return out


def build(nc, pairs, x, txt, edges, plain, split, rows, const, out):
    ctx = ExitStack()
    with ctx:
        def sb(name, shape, dt, where=ctx):
            return where.enter_context(nc.sbuf_tensor(name, shape, dt))

        def sem(name):
            return ctx.enter_context(nc.semaphore(name))

        ps = ctx.enter_context(nc.psum_tensor("ps", [128, 8, 512], F32))
        place = {"T0": ps[:, 0:2, :], "T1": ps[:, 2:4, :], "T2": ps[:, 4:6, :],
                 "B6": ps[:, 6, :], "B7": ps[:, 7, :]}
        ps_bf = ps[:, 6, :].bitcast(BF16)

        W = sb("plain_w", [128, PLAIN_W], F32)
        WH = sb("split_hi", [128, SPLIT_W], F32R)
        WL = sb("split_lo", [128, SPLIT_W], F32R)
        RW = sb("bias_rows", [128, ROWS_W], F32)
        ident = sb("ident", [128, 128], F32)
        ident_bf = sb("ident_bf", [128, 128], BF16)
        before = sb("before", [128, 16], F32)
        wo3 = sb("wo_parts", [64, 3, 64], BF16)
        posb = sb("pos_and_bias", [128, PATCHES], F32)
        dinv = sb("dinv_row", [128, PATCHES], F32)
        adj = sb("adjacency", [GBLK, NG, PATCHES], F32R)

        def w(name, i=0, n=None):
            a, z = PLAIN[name]
            n = n or z - a
            return W[:, a + i * n:a + (i + 1) * n]

        def wsplit(tile, name, i=0, n=None):
            a, z = SPLIT[name]
            n = n or z - a
            return tile[:, a + i * n:a + (i + 1) * n]

        def row(name, i=0, n=64):
            a, _ = ROWS[name]
            return RW[0:BLK, a + i * n:a + (i + 1) * n]

        load_sem = sem("setup_load")
        const_sem = sem("setup_iota")
        init_v = sem("setup_vector")
        init_p = sem("setup_pool")
        hot_sem = sem("setup_onehot")
        cnt_full = sem("setup_counts_full")
        cnt_free = sem("setup_counts_free")
        deg_full = sem("setup_degree_full")
        root_sem = sem("setup_root")
        with ExitStack() as tmp:
            raw = sb("split_raw", [128, SPLIT_W], F32, tmp)
            iota = sb("iota", [128, PATCHES], F32, tmp)
            e_int = sb("edges_int", [ECH, 2, NEC], I32, tmp)
            e_f = sb("edges_f", [ECH, 2, NEC], F32, tmp)
            hot_s = sb("onehot_src", [ECH, NEC, PATCHES], BF16, tmp)
            hot_d = sb("onehot_dst", [ECH, NEC, PATCHES], BF16, tmp)
            ones = sb("ones", [ECH, 128], BF16, tmp)
            slide = sb("ident_slide", [GBLK, 2 * PATCHES + GBLK], BF16, tmp)
            deg = sb("degree", [128, PATCHES], F32, tmp)
            tmp1 = sb("newton", [128, PATCHES], F32, tmp)
            wor = sb("wo_rest", [64, 2, 64], F32, tmp)
            with nc.Block() as block:
                @block.sync
                def _(sp):
                    c = CONST
                    sp.dma_start(iota[:, :], const[:, c["iota"][0]:c["iota"][1]]).then_inc(const_sem, 16)
                    sp.dma_start(e_int[:, :, :], edges.rearrange("s (p c) -> p s c", p=ECH)
                                 ).then_inc(const_sem, 16)
                    sp.dma_start(W[:, :], plain).then_inc(load_sem, 16)
                    sp.dma_start(raw[:, :], split).then_inc(load_sem, 16)
                    sp.dma_start(RW[:, :], rows.to_broadcast([128, ROWS_W])).then_inc(load_sem, 16)
                    sp.dma_start(ident[:, :], const[:, c["ident"][0]:c["ident"][1]]).then_inc(load_sem, 16)
                    sp.dma_start(posb[:, :], const[:, c["pos"][0]:c["pos"][1]]).then_inc(load_sem, 16)
                    sp.dma_start(before[:, :], const[:, c["before"][0]:c["before"][1]]).then_inc(load_sem, 16)

                @block.gpsimd
                def _(pool):
                    pool.memset(ones[:, :], 1.0).then_inc(init_p, 1)
                    pool.memset(slide[:, :], 0.0).then_inc(init_p, 1)

                @block.vector
                def _(v):
                    done = [0]

                    def settle(ins):
                        done[0] += 1
                        ins.then_inc(init_v, 1)
                        v.wait_ge(init_v, done[0])

                    v.wait_ge(const_sem, 32)
                    settle(v.tensor_copy(e_f[:, :, :], e_int[:, :, :]))
                    for c in range(NEC):
                        v.tensor_scalar(hot_s[:, c, :], iota[0:ECH, :], e_f[:, 0, c:c + 1], None,
                                        ALU.is_equal).then_inc(hot_sem, 1)
                        v.tensor_scalar(hot_d[:, c, :], iota[0:ECH, :], e_f[:, 1, c:c + 1], None,
                                        ALU.is_equal).then_inc(hot_sem, 1)
                    v.wait_ge(load_sem, 96)
                    v.tensor_copy(ident_bf[:, :], ident[:, :])
                    v.wait_ge(init_p, 2)
                    settle(v.tensor_copy(slide[:, PATCHES:PATCHES + GBLK], ident[0:GBLK, 0:GBLK]))
                    settle(v.tensor_copy(WH[:, :], raw[:, :]))
                    v.tensor_tensor(WL[:, :], raw[:, :], WH[:, :].bitcast(F32), ALU.subtract)
                    settle(v.tensor_copy(wo3[:, 0, :], w("wo")[0:64, :]))
                    settle(v.tensor_tensor(wor[:, 0, :], w("wo")[0:64, :], wo3[:, 0, :], ALU.subtract))
                    settle(v.tensor_copy(wo3[:, 1, :], wor[:, 0, :]))
                    settle(v.tensor_tensor(wor[:, 1, :], wor[:, 0, :], wo3[:, 1, :], ALU.subtract))
                    v.tensor_copy(wo3[:, 2, :], wor[:, 1, :])
                    v.tensor_scalar(posb[:, :], posb[:, :], w("b_emb"), None, ALU.add)
                    v.wait_ge(deg_full, 1)
                    v.tensor_scalar(deg[:, :].rearrange("p (a n) -> p a n", a=2), ps[:, 6:8, 0:GHALF], 1.0, None,
                                    ALU.add).then_inc(root_sem, 1)
                    v.wait_ge(root_sem, 2)
                    settle(v.reciprocal(dinv[:, :], tmp1[:, :]))
                    settle(v.tensor_tensor(tmp1[:, :], dinv[:, :], dinv[:, :], ALU.mult))
                    settle(v.tensor_tensor(tmp1[:, :], tmp1[:, :], deg[:, :], ALU.mult))
                    settle(v.tensor_scalar(tmp1[:, :], tmp1[:, :], -0.5, 1.5, ALU.mult, ALU.add))
                    settle(v.tensor_tensor(dinv[:, :], dinv[:, :], tmp1[:, :], ALU.mult))

                @block.scalar
                def _(a):
                    a.wait_ge(root_sem, 1)
                    a.activation(tmp1[:, :], deg[:, :], ACT.Sqrt).then_inc(root_sem, 1)
                    for n in range(2 * NG):
                        half, sblk = n // NG, n % NG
                        a.wait_ge(cnt_full, n + 1)
                        a.activation(adj[:, sblk, half * GHALF:(half + 1) * GHALF], ps[0:GBLK, n % 6, 0:GHALF],
                                     ACT.Copy).then_inc(cnt_free, 1)

                @block.tensor
                def _(pe):
                    pe.wait_ge(hot_sem, 2 * NEC)
                    pe.wait_ge(init_p, 2)
                    for c in range(NEC):
                        for half in range(2):
                            mm = pe.matmul(ps[:, 6 + half, 0:GHALF], ones[:, :],
                                           hot_d[:, c, half * GHALF:(half + 1) * GHALF],
                                           start=c == 0, stop=c == NEC - 1)
                    mm.then_inc(deg_full, 1)
                    pe.wait_ge(init_v, 2)
                    for n in range(2 * NG):
                        half, sblk = n // NG, n % NG
                        if n >= 6:
                            pe.wait_ge(cnt_free, n - 5)
                        at = PATCHES - sblk * GBLK + half * GHALF
                        pe.matmul(ps[0:GBLK, n % 6, 0:GHALF], slide[:, PATCHES:PATCHES + GBLK],
                                  slide[:, at:at + GHALF], start=True, stop=False)
                        for c in range(NEC):
                            mm = pe.matmul(ps[0:GBLK, n % 6, 0:GHALF], hot_s[:, c, sblk * GBLK:(sblk + 1) * GBLK],
                                           hot_d[:, c, half * GHALF:(half + 1) * GHALF],
                                           start=False, stop=c == NEC - 1)
                        mm.then_inc(cnt_full, 1)

        X = sb("image_rows", [96, GRID // 2, GRID * PATCH], F32)
        HT = sb("nodes_T", [128, PATCHES], F32)
        parts = [sb(n, [128, NG * 128], F32R) for n in ("parts_hi", "parts_lo")]
        UH, UL = (p[0:GBLK, :].rearrange("p (k n) -> p k n", n=128) for p in parts)
        QKH, QKL = (p[:, 0:COLS] for p in parts)
        HN = sb("tokens_next", [BLK, NB, 2, HID], F32)
        H = sb("tokens", [BLK, NB, 2, HID], F32)
        XC = sb("centred", [BLK, NB, HID], F32)
        SQ = sb("squared", [BLK, NB, HID], F32)
        XN = {k: sb(f"normed_twice_{k}", [BLK, NB, 2, HID], F32) for k in "am"}
        st7 = sb("ln_stats", [BLK, 4, NB], F32)
        halfneg = sb("minus_half", [BLK, NB], F32)
        XS = {"a": sb("x_stack_attn", [128, COLS], F32R), "m": sb("x_stack_moe", [128, COLS], F32R)}
        QS = sb("q_stack", [SHIFT_ROW + 1, 2, HEADS, COLS], F32R)
        KS = sb("k_stack", [SHIFT_ROW + 1, 2, HEADS, COLS], F32R)
        VV = sb("v_and_one", [BLK, 2, NB, HEADS, 32], F32)
        P = sb("probs", [128, 2, HEADS, 2, HW], F32)
        NM = sb("neg_max_halves", [BLK, NB * HEADS, 2], F32)
        NMM = sb("neg_max", [BLK, NB * HEADS], F32)
        MR = sb("neg_max_rows", [HEADS, COLS], F32R)
        OT = sb("attn_T", [128, COLS], F32)
        RC = sb("inv_sums", [BLK, NB, HEADS], F32)
        OB = sb("attn_bf", [BLK, NB, HEADS, HD], BF16)
        OBT = sb("attn_bf_T", [64, NB, BLK + 1], BF16)
        OT2 = sb("moe_T", [128, 4 * BLK], F32)
        GZ = sb("gate_vals", [BLK, 4, NB, EXPERTS], F32)
        GS = sb("gate_sums", [BLK, 2, NB], F32)
        GC = sb("gate_cmp", [BLK, 2, NB, EXPERTS, EXPERTS], F32)
        GW = sb("gate_weights", [BLK, NB, EXPERTS], F32)
        GWW = sb("gate_weights_wide", [BLK, NB, EXPERTS, HID], F32)
        TMP = sb("bias_term", [BLK, NB, HID], F32)
        OUTT = sb("out_tile", [BLK, NB, HID], F32)

        flatP = P[:, :, :, :, :].rearrange("p a h t n -> p (a h t n)")
        H1 = [flatP[:, e * COLS:(e + 1) * COLS] for e in range(5)]
        H2 = [flatP[:, 5 * COLS + j * TOKENS:5 * COLS + (j + 1) * TOKENS] for j in range(3)]

        def halves(ap):
            return ap.rearrange("p (t n) -> p t n", t=2)

        scratch = nc.dram_tensor("qk_scratch", (2, 2, 2, HEADS, HD, COLS), F32, kind="Internal").ap()

        full = {r: sem(f"{r}_full") for r in place}
        free = {r: sem(f"{r}_free") for r in place}
        x_dma, txt_dma = sem("x_dma"), sem("txt_dma")
        hcopied = sem("tokens_copied")
        ht_scaled, ht_relu = sem("ht_scaled"), sem("ht_relu")
        centred, squared, var_ready, rstd_ready, normed = (sem(n) for n in
                                                           ("centred_s", "squared_s", "var_ready", "rstd_ready", "normed_s"))
        xt_hi, qk_hi, stack_dma, nm_ready, mrow_dma = (
            sem(n) for n in ("xt_hi", "qk_hi_s", "stack_dma", "nm_ready", "mrow_dma"))
        pv_done = sem("pv_done")
        g_sub, g_exp, g_prob, g_exp2, g_weight, hb_ready = (
            sem(n) for n in ("g_sub", "g_exp", "g_prob", "g_exp2", "g_weight", "hb_ready"))
        out_dma, g_wide, scratch_dma = sem("out_dma"), sem("g_wide"), sem("scratch_dma")
        v_chain, p_chain = sem("v_chain"), sem("p_chain")
        round_sems = [*full.values(), *free.values(), x_dma, txt_dma, hcopied, ht_scaled, ht_relu, centred, squared,
                      var_ready, rstd_ready, normed, xt_hi, qk_hi, stack_dma, nm_ready, mrow_dma, pv_done, g_sub,
                      g_exp, g_prob, g_exp2, g_weight, hb_ready, out_dma, g_wide, scratch_dma, v_chain, p_chain]
        arrived = sem("arrived")
        numbers = [s.num for s in (*round_sems, arrived)]
        assert sorted(numbers) == list(range(min(numbers), max(numbers) + 1))
        go = sem("go")

        def read(eng, turn, st):
            r, n = turn[st]
            eng.wait_ge(free[r], n)

        prologue, middle, last = prologue_steps(), round_steps(True), round_steps(False)

        def rounds(eng, run, end):
            run(prologue, None)
            end(1)
            if pairs > 1:
                with eng.Fori(0, pairs - 1) as i:
                    run(middle, i)
                    end(i + 2)
            run(last, pairs - 1)

        def report(eng):
            def end(n):
                eng.drain().then_inc(arrived, 1)
                eng.wait_ge(go, n)
            return end

        block = ctx.enter_context(nc.Block())

        @block.sync
        def _(sp):
            def run(steps, i):
                turn, nth = turns(steps), ordinal(steps)
                has_next = ("embed", 0) in turn
                nxt = 0 if i is None else i + 1
                if i is None:
                    sp.wait_ge(v_chain, 1)
                if has_next:
                    if i is not None:
                        sp.wait_ge(hcopied, 1)
                    for b in range(2):
                        sp.dma_start(HN[PATCHES - 6 * BLK:BLK, NB - 1, b, :],
                                     txt[bass.ds(nxt * 2 + b, 1), :, :].rearrange("o t f -> (o t) f")
                                     ).then_inc(txt_dma, 16)
                for st in steps:
                    kind = st[0]
                    if kind == "hcopy" or (i is None and st == ("embed", 0)):
                        if has_next:
                            load_rows(nxt, 0)
                    if kind == "embed" and st[1] == 0:
                        r, n = turn[st]
                        sp.wait_ge(full[r], n)
                        load_rows(nxt, 1)
                    elif kind == "v":
                        b, rq, nq = st[1], *turn[("qk", st[1])]
                        sp.wait_ge(qk_hi, nth[("qk", b)])
                        sp.wait_ge(free[rq], nq)
                        for part, tile in enumerate((QKH, QKL)):
                            sp.dma_start(scratch[b, part].rearrange("a h r c -> (a h r) c"), tile.bitcast(F32)
                                         ).then_inc(scratch_dma, 16)
                        sp.wait_ge(scratch_dma, 32 * nth[("qk", b)])
                        for part in range(2):
                            q_part = scratch[b, part, 0].rearrange("h r c -> r h c")
                            k_part = scratch[b, part, 1].rearrange("h r c -> r h c")
                            for copy in range(2):
                                rq, rk = HD * (2 * copy + part), HD * (2 * part + copy)
                                sp.dma_start(QS[rq:rq + HD, b, :, :].bitcast(F32), q_part).then_inc(stack_dma, 16)
                                sp.dma_start(KS[rk:rk + HD, b, :, :].bitcast(F32), k_part).then_inc(stack_dma, 16)
                    elif kind == "mrow" and st[2] == 1:
                        read(sp, turn, ("mrow", st[1], 0))
                        read(sp, turn, st)
                        for h in range(HEADS):
                            sp.dma_start(QS[SHIFT_ROW:SHIFT_ROW + 1, st[1], h, :].bitcast(F32), MR[h:h + 1, :].bitcast(F32)
                                         ).then_inc(mrow_dma, 16)
                    elif kind == "back":
                        read(sp, turn, st)
                        dst = out[bass.ds(i * 2 + st[1], 1), :, :].rearrange("o (n p) f -> (o p) n f", p=BLK)
                        sp.dma_start(dst, OUTT[:, :, :]).then_inc(out_dma, 16)
                if has_next:
                    sp.wait_ge(x_dma, 2 * X_LOADS)
                    sp.wait_ge(txt_dma, 32)
                if i is not None:
                    sp.wait_ge(out_dma, 32)
                if has_next:
                    sp.wait_ge(stack_dma, 2 * STACK_LOADS)
                sp.wait_ge(mrow_dma, 64 * sum(s[0] == "mrow" for s in steps) // 2)

            def load_rows(nxt, half):
                rows = GRID * PATCH // 2
                for b in range(2):
                    for c in range(CH):
                        src = x[bass.ds(nxt * 2 + b, 1), c, half * rows:(half + 1) * rows, :]
                        p = (b * CH + c) * PATCH
                        sp.dma_start(X[p:p + PATCH, :, :], src.rearrange("o (i q) w -> (o q) i w", q=PATCH)
                                     ).then_inc(x_dma, 16)

            def end(n):
                sp.wait_ge(arrived, 4)
                sp.sem_clear(range(min(numbers), max(numbers) + 1))
                sp.sem_inc(go, 1)

            rounds(sp, run, end)

        @block.gpsimd
        def _(pool):
            chain = [0]

            def settle(ins):
                chain[0] += 1
                ins.then_inc(p_chain, 1)
                pool.wait_ge(p_chain, chain[0])

            def run(steps, i):
                chain[0] = 0
                turn, nth = turns(steps), ordinal(steps)
                if i is None:
                    settle(pool.memset(halfneg[:, :], -0.5))
                    for tile in (XS["a"], XS["m"], MR):
                        settle(pool.memset(tile[:, TOKENS:COLS].bitcast(F32), 0.0))
                    settle(pool.memset(VV[:, :, :, :, :], 0.0))
                    settle(pool.memset(VV[:, :, :, :, HD:HD + 1], 1.0))
                    settle(pool.memset(QS[64:SHIFT_ROW, :, :, :].bitcast(F32), 0.0))
                    settle(pool.memset(KS[64:SHIFT_ROW, :, :, :].bitcast(F32), 0.0))
                    settle(pool.memset(KS[SHIFT_ROW:SHIFT_ROW + 1, :, :, :].bitcast(F32), 1.0))
                for st in steps:
                    kind = st[0]
                    if kind == "hcopy":
                        pool.tensor_copy(H[:, :, :, :], HN[:, :, :, :]).then_inc(hcopied, 1)
                    elif kind == "embed":
                        c = slice(st[1] * GHALF, (st[1] + 1) * GHALF)
                        read(pool, turn, st)
                        pool.tensor_tensor(HT[:, c], HT[:, c], dinv[:, c], ALU.mult).then_inc(ht_scaled, 1)
                    elif kind == "gagg" and st[1] < 2:
                        c = slice(st[2] * GHALF, (st[2] + 1) * GHALF)
                        pool.wait_ge(ht_relu, nth[st])
                        pool.tensor_tensor(HT[:, c], HT[:, c], dinv[:, c], ALU.mult).then_inc(ht_scaled, 1)
                    elif kind == "ln":
                        n = nth[st]
                        pool.wait_ge(var_ready, n)
                        pool.tensor_tensor(st7[:, 3, :], st7[:, 2, :], halfneg[:, :], ALU.pow).then_inc(rstd_ready, 1)
                    elif kind == "hb":
                        b = st[1]
                        pool.wait_ge(g_weight, nth[st])
                        hb = H[:, :, b, :]
                        shape = [BLK, NB, HID]
                        settle(pool.tensor_tensor(hb, hb, row("sb3").unsqueeze(1).to_broadcast(shape), ALU.add))
                        for e in range(EXPERTS):
                            settle(pool.tensor_tensor(TMP[:, :, :], GW[:, :, e:e + 1].to_broadcast(shape),
                                                      row("eb3", e).unsqueeze(1).to_broadcast(shape), ALU.mult))
                            ins = pool.tensor_tensor(hb, hb, TMP[:, :, :], ALU.add)
                            if e < EXPERTS - 1:
                                settle(ins)
                        ins.then_inc(hb_ready, 1)

            rounds(pool, run, report(pool))

        @block.scalar
        def _(act):
            def run(steps, i):
                turn, nth = turns(steps), ordinal(steps)
                for st in steps:
                    kind = st[0]
                    r, n = turn.get(st, (None, 0))
                    if r:
                        T = place[r]
                    if kind == "s":
                        _, b, kb, h = st
                        act.wait_ge(full[r], n)
                        if h == 0 and kb >= 2:
                            act.wait_ge(pv_done, b * (2 * NB - 1) + 2 * (kb - 1))
                        elif h == 0 and b == 1:
                            act.wait_ge(full["T2"], 1)
                        act.activation(P[0:BLK, kb % 2, h, :, :], T[0:BLK, :, 0:HW], ACT.Exp,
                                       scale=SCALE).then_inc(free[r], 1)
                    elif kind == "gw" and st[1] < 3:
                        half = st[2]
                        blocks = range(4) if half == 0 else range(4, NG)
                        act.wait_ge(full[r], n)
                        act.activation(UH[:, blocks[0]:blocks[-1] + 1, :].rearrange("p k n -> p (k n)"),
                                       T[0:GBLK, 0:128 * len(blocks)], ACT.Copy).then_inc(xt_hi, 1)
                    elif kind == "gagg":
                        c = slice(st[2] * GHALF, (st[2] + 1) * GHALF)
                        read(act, turn, st)
                        act.activation(HT[:, c], HT[:, c], ACT.Relu, bias=w("b_gcn", st[1], 1)).then_inc(ht_relu, 1)
                    elif kind == "xt":
                        act.wait_ge(full[r], n)
                        if st[2] == "a" and nth.get(("v", st[1]), 1) > 1:
                            rv, nv = turn[("v", 1 - st[1])]
                            act.wait_ge(full[rv], nv)
                        for t, (c0, cn) in enumerate(PIECES):
                            ins = act.activation(XS[st[2]][:, c0:c0 + cn], T[:, t, 0:cn], ACT.Copy)
                        ins.then_inc(xt_hi, 1)
                    elif kind == "qk":
                        act.wait_ge(full[r], n)
                        if nth[st] > 1:
                            act.wait_ge(stack_dma, STACK_LOADS * (nth[st] - 1))
                        act.activation(halves(QKH), T[:, :, 0:HW], ACT.Identity,
                                       bias=w("b_qk")).then_inc(qk_hi, 1)
                    elif kind == "mrow":
                        c0, cn = PIECES[st[2]]
                        act.wait_ge(full[r], n)
                        if nth[st] > 2:
                            act.wait_ge(mrow_dma, 64 * ((nth[st] - 1) // 2))
                        act.activation(MR[:, c0:c0 + cn], T[0:HEADS, 0:cn], ACT.Copy).then_inc(free[r], 1)
                    elif kind == "oev":
                        rv, nv = turn[("pv", st[1], 0, 0)]
                        act.wait_ge(full[rv], nv)
                        act.activation(halves(OT[:, :]), place[rv][:, :, 0:HW], ACT.Copy).then_inc(free[rv], 1)
                    elif kind == "obt":
                        act.wait_ge(full[r], n)
                        act.activation(OBT[:, :, 0:BLK],
                                       ps_bf[0:64, 0:NB * (BLK + 1)].rearrange("p (k n) -> p k n", k=NB)[:, :, 0:BLK],
                                       ACT.Copy).then_inc(free[r], 1)
                    elif kind == "ln":
                        act.wait_ge(centred, nth[st])
                        act.activation(SQ[:, :, :], XC[:, :, :], ACT.Square).then_inc(squared, 1)
                    elif kind == "g3":
                        act.wait_ge(g_weight, nth[st])
                        act.activation(GWW[:, :, :, :], GW[:, :, :].unsqueeze(3).to_broadcast([BLK, NB, EXPERTS, HID]),
                                       ACT.Copy).then_inc(g_wide, 1)
                    elif kind == "gate":
                        act.wait_ge(g_sub, nth[st])
                        act.activation(GZ[:, 1, :, :], GZ[:, 0, :, :], ACT.Exp).then_inc(g_exp, 1)
                    elif kind == "g2":
                        act.wait_ge(g_prob, nth[st])
                        act.activation(GZ[:, 3, :, :], GZ[:, 2, :, :], ACT.Exp).then_inc(g_exp2, 1)
                    elif kind == "l1":
                        e = st[2]
                        bias = w("eb1", e, 1) if e < EXPERTS else w("sb1")
                        act.wait_ge(full[r], n)
                        act.activation(halves(H1[e]), T[:, :, 0:HW], ACT.Relu, bias=bias).then_inc(free[r], 1)
                    elif kind == "l2":
                        j = st[2]
                        bias = w("eb2", j, 1) if j < 2 else w("sb2")
                        act.wait_ge(full[r], n)
                        for t, (c0, cn) in enumerate(PIECES):
                            ins = act.activation(H2[j][:, c0:c0 + cn], T[:, t, 0:cn], ACT.Relu, bias=bias)
                        ins.then_inc(free[r], 1)
                    elif kind == "l3":
                        act.wait_ge(full[r], n)
                        act.activation(OT2[0:64, 0:4 * BLK], T[0:64, 0, 0:4 * BLK], ACT.Copy)
                        act.activation(OT2[64:128, 0:3 * BLK], T[64:128, 0, 0:3 * BLK], ACT.Copy).then_inc(free[r], 1)

            rounds(act, run, report(act))

        @block.vector
        def _(v):
            chain = [0]

            def settle(ins):
                chain[0] += 1
                ins.then_inc(v_chain, 1)
                v.wait_ge(v_chain, chain[0])

            def run(steps, i):
                chain[0] = 0
                turn, nth = turns(steps), ordinal(steps)
                if i is None:
                    settle(v.memset(X[:, :, :], 0.0))
                    v.wait_ge(p_chain, 9)
                hi_no = {}
                for st in steps:
                    if st[0] == "xt" or (st[0] == "gw" and st[1] < 3):
                        hi_no[st] = len(hi_no) + 1
                for st in steps:
                    kind = st[0]
                    r, n = turn.get(st, (None, 0))
                    if r:
                        T = place[r]
                    if kind == "mx":
                        _, b, qb, h, half = st
                        v.wait_ge(full[r], n)
                        keys = min(HW, TOKENS - half * HW)
                        v.tensor_reduce(NM[:, qb * HEADS + h, half:half + 1], T[0:BLK, 0:keys], AX.X, ALU.max,
                                        negate=True).then_inc(free[r], 1)
                        if (qb, h, half) == (NB - 1, HEADS - 1, 1):
                            v.wait_ge(free[r], n)
                            v.tensor_reduce(NMM[:, :], NM[:, :, :], AX.X, ALU.min).then_inc(nm_ready, 1)
                    elif kind == "embed":
                        c = slice(st[1] * GHALF, (st[1] + 1) * GHALF)
                        v.wait_ge(full[r], n)
                        v.tensor_tensor(HT[:, c], T[:, 0:GHALF], posb[:, c], ALU.add).then_inc(free[r], 1)
                    elif kind == "gw" and st[1] < 3:
                        half = st[2]
                        blocks = range(4) if half == 0 else range(4, NG)
                        k = slice(blocks[0], blocks[-1] + 1)
                        v.wait_ge(xt_hi, hi_no[st])
                        v.tensor_tensor(UL[:, k, :], T[0:GBLK, 0:128 * len(blocks)].rearrange("p (k n) -> p k n", n=128),
                                        UH[:, k, :].bitcast(F32), ALU.subtract).then_inc(free[r], 1)
                    elif kind == "gw":
                        v.wait_ge(full[r], n)
                        if i is not None:
                            v.wait_ge(hcopied, 1)
                        bias = row("b_out")
                        jobs = [(0, 4, BLK)] if st[2] == 0 else [(4, 2, BLK), (6, 1, PATCHES - 6 * BLK)]
                        for k0, kn, np_ in jobs:
                            o = (k0 - 4 * st[2]) * 128
                            ins = v.tensor_tensor(
                                HN[0:np_, k0:k0 + kn, :, :].rearrange("p k b f -> p (k b) f"),
                                T[0:np_, o:o + kn * 128].rearrange("p (k f) -> p k f", f=HID),
                                bias[0:np_, :].unsqueeze(1).to_broadcast([np_, kn * 2, HID]), ALU.add)
                        ins.then_inc(free[r], 1)
                    elif kind == "gagg":
                        c = slice(st[2] * GHALF, (st[2] + 1) * GHALF)
                        v.wait_ge(full[r], n)
                        v.tensor_tensor(HT[:, c], T[:, 0:GHALF], dinv[:, c], ALU.mult).then_inc(free[r], 1)
                    elif kind == "ln":
                        _, b, which = st
                        src = (HN if which == "a" else H)[:, :, b, :]
                        shape = [BLK, NB, HID]
                        m = nth[st]
                        if which == "a":
                            rg, ng = turn.get(("gw", 3, 1), (None, 0))
                            v.wait_ge(free[rg], ng)
                            v.wait_ge(txt_dma, 32)
                        settle(v.tensor_reduce(st7[:, 0, :], src, AX.X, ALU.add))
                        settle(v.tensor_scalar(st7[:, 0, :], st7[:, 0, :], 1.0 / HID, None, ALU.mult))
                        v.tensor_tensor(XC[:, :, :], src, st7[:, 0, :].unsqueeze(2).to_broadcast(shape),
                                        ALU.subtract).then_inc(centred, 1)
                        v.wait_ge(squared, m)
                        settle(v.tensor_reduce(st7[:, 1, :], SQ[:, :, :], AX.X, ALU.add))
                        v.tensor_scalar(st7[:, 2, :], st7[:, 1, :], 1.0 / HID, EPS, ALU.mult, ALU.add
                                        ).then_inc(var_ready, 1)
                        v.wait_ge(rstd_ready, m)
                        twice = [BLK, NB, 2, HID]
                        v.tensor_tensor(XN[which][:, :, :, :], XC[:, :, :].unsqueeze(2).to_broadcast(twice),
                                        st7[:, 3, :].unsqueeze(2).unsqueeze(3).to_broadcast(twice),
                                        ALU.mult).then_inc(normed, 1)
                    elif kind == "xt":
                        v.wait_ge(xt_hi, hi_no[st])
                        tile = XS[st[2]]
                        for t, (c0, cn) in enumerate(PIECES):
                            ins = v.tensor_tensor(tile[64:128, c0:c0 + cn], T[64:128, t, 0:cn],
                                                  tile[64:128, c0:c0 + cn].bitcast(F32), ALU.subtract)
                        ins.then_inc(free[r], 1)
                    elif kind == "qk":
                        v.wait_ge(qk_hi, nth[st])
                        if nth[st] > 1:
                            v.wait_ge(stack_dma, STACK_LOADS * (nth[st] - 1))
                        v.scalar_tensor_tensor(out=halves(QKL), in0=T[:, :, 0:HW], scalar=w("b_qk"),
                                               in1=halves(QKH).bitcast(F32), op0=ALU.add, op1=ALU.subtract
                                               ).then_inc(free[r], 1)
                    elif kind == "v":
                        b = st[1]
                        v.wait_ge(full[r], n)
                        for k0, kn in ((0, NB),):
                            ins = v.tensor_tensor(
                                VV[:, b, :, :, 0:HD],
                                T[0:BLK, 0, 0:NB * HID].rearrange("p (k h d) -> p k h d", h=HEADS, d=HD),
                                row("bv").rearrange("p (h d) -> p h d", h=HEADS).unsqueeze(1)
                                .to_broadcast([BLK, NB, HEADS, HD]), ALU.add)
                        ins.then_inc(free[r], 1)
                    elif kind == "ot":
                        _, b, part = st
                        k0, kn = (0, 4) if part == 0 else (4, 3)
                        v.wait_ge(full[r], n)
                        t4 = T[0:BLK, 0:kn * 128].rearrange("p (k h d) -> p k h d", h=HEADS, d=32)
                        settle(v.reciprocal(RC[:, k0:k0 + kn, :], t4[:, :, :, HD]))
                        v.tensor_tensor(OB[:, k0:k0 + kn, :, :], t4[:, :, :, 0:HD],
                                        RC[:, k0:k0 + kn, :].unsqueeze(3).to_broadcast([BLK, kn, HEADS, HD]),
                                        ALU.mult).then_inc(free[r], 1)
                    elif kind == "wo":
                        b = st[1]
                        v.wait_ge(full[r], n)
                        v.wait_ge(hcopied, 1)
                        hb = H[:, :, b, :]
                        ins = v.tensor_tensor(hb, T[0:BLK, 0:NB * HID].rearrange("p (k f) -> p k f", f=HID), hb, ALU.add)
                        ins.then_inc(free[r], 1)
                        v.wait_ge(free[r], n)
                        settle(v.tensor_tensor(hb, hb, row("bo").unsqueeze(1).to_broadcast([BLK, NB, HID]), ALU.add))
                    elif kind == "gate":
                        v.wait_ge(full[r], n)
                        sh = [BLK, NB, EXPERTS]
                        ins = v.tensor_tensor(GZ[:, 0, :, :], T[0:BLK, 0, 0:NB * EXPERTS].rearrange("p (k e) -> p k e", e=EXPERTS),
                                              row("gb", 0, EXPERTS).unsqueeze(1).to_broadcast(sh), ALU.add)
                        ins.then_inc(free[r], 1)
                        v.wait_ge(free[r], n)
                        settle(v.tensor_reduce(GS[:, 0, :], GZ[:, 0, :, :], AX.X, ALU.max))
                        v.tensor_tensor(GZ[:, 0, :, :], GZ[:, 0, :, :], GS[:, 0, :].unsqueeze(2).to_broadcast(sh),
                                        ALU.subtract).then_inc(g_sub, 1)
                    elif kind == "g2":
                        sh = [BLK, NB, EXPERTS]
                        sh4 = [BLK, NB, EXPERTS, EXPERTS]
                        v.wait_ge(g_exp, nth[st])
                        settle(v.tensor_reduce(GS[:, 0, :], GZ[:, 1, :, :], AX.X, ALU.add))
                        settle(v.reciprocal(GS[:, 1, :], GS[:, 0, :]))
                        v.tensor_tensor(GZ[:, 2, :, :], GZ[:, 1, :, :], GS[:, 1, :].unsqueeze(2).to_broadcast(sh),
                                        ALU.mult).then_inc(g_prob, 1)
                        v.wait_ge(g_prob, nth[st])
                        pi = GZ[:, 2, :, :].unsqueeze(3).to_broadcast(sh4)
                        pj = GZ[:, 2, :, :].unsqueeze(2).to_broadcast(sh4)
                        v.tensor_tensor(GC[:, 0, :, :, :], pj, pi, ALU.is_gt)
                        settle(v.tensor_tensor(GC[:, 1, :, :, :], pj, pi, ALU.is_equal))
                        mask = before[0:BLK, :].rearrange("p (i j) -> p i j", i=EXPERTS).unsqueeze(1).to_broadcast(sh4)
                        settle(v.tensor_tensor(GC[:, 1, :, :, :], GC[:, 1, :, :, :], mask, ALU.mult))
                        settle(v.tensor_tensor(GC[:, 0, :, :, :], GC[:, 0, :, :, :], GC[:, 1, :, :, :], ALU.add))
                        settle(v.tensor_reduce(GZ[:, 0, :, :], GC[:, 0, :, :, :], AX.X, ALU.add))
                    elif kind == "g3":
                        sh = [BLK, NB, EXPERTS]
                        v.wait_ge(g_exp2, nth[st])
                        settle(v.scalar_tensor_tensor(out=GZ[:, 1, :, :], in0=GZ[:, 0, :, :], scalar=1.5,
                                                      in1=GZ[:, 3, :, :], op0=ALU.is_lt, op1=ALU.mult))
                        settle(v.tensor_reduce(GS[:, 0, :], GZ[:, 1, :, :], AX.X, ALU.add))
                        settle(v.reciprocal(GS[:, 1, :], GS[:, 0, :]))
                        v.tensor_tensor(GW[:, :, :], GZ[:, 1, :, :], GS[:, 1, :].unsqueeze(2).to_broadcast(sh),
                                        ALU.mult).then_inc(g_weight, 1)
                    elif kind == "wb":
                        _, b, j = st
                        v.wait_ge(full[r], n)
                        rl, nl = turn[("l2", b, j)]
                        v.wait_ge(free[rl], nl)
                        for t, (c0, cn) in enumerate(PIECES):
                            ins = v.tensor_tensor(H2[j][:, c0:c0 + cn], T[:, t, 0:cn], H2[j][:, c0:c0 + cn], ALU.mult)
                        ins.then_inc(free[r], 1)
                    elif kind == "back":
                        _, b = st
                        v.wait_ge(full[r], n)
                        v.wait_ge(hb_ready, nth[st])
                        if nth[st] > 1:
                            v.wait_ge(out_dma, 16 * (nth[st] - 1))
                        for t, (k0, kn) in enumerate(((0, 4), (4, 3))):
                            ins = v.tensor_tensor(
                                OUTT[:, k0:k0 + kn, :], T[0:BLK, t, 0:kn * HID].rearrange("p (k f) -> p k f", f=HID),
                                H[:, k0:k0 + kn, b, :], ALU.add)
                        ins.then_inc(free[r], 1)

            rounds(v, run, report(v))

        @block.tensor
        def _(pe):
            def run(steps, i):
                turn, nth = turns(steps), ordinal(steps)
                if i is None:
                    pe.wait_ge(p_chain, 9)
                for st in steps:
                    kind = st[0]
                    r, n = turn.get(st, (None, 0))
                    if r:
                        T = place[r]
                        if n > 1:
                            pe.wait_ge(free[r], n - 1)
                    mm = None
                    if kind == "s":
                        _, b, kb, h = st
                        if b == 1 and (kb, h) == (0, 0):
                            pe.wait_ge(mrow_dma, 64)
                        for t, (c0, cn) in enumerate(HALVES):
                            mm = pe.matmul(T[0:BLK, t, 0:cn], KS[:, b, h, kb * BLK:(kb + 1) * BLK],
                                           QS[:, b, h, c0:c0 + cn], start=True, stop=True)
                    elif kind == "pv":
                        _, b, kb, t = st
                        T2 = place["T2"]
                        if t == 0:
                            for h in (2, 3):
                                read(pe, turn, ("s", b, kb, h))
                        for h in range(HEADS):
                            pm = pe.matmul(T2[32 * h:32 * h + 32, t, 0:HW], VV[:, b, kb, h, :],
                                           P[0:BLK, kb % 2, h, t, :], start=kb == 0, stop=kb == NB - 1,
                                           tile_position=(0, 32 * h))
                        if (kb, t) == (NB - 1, 1):
                            pm.then_inc(full["T2"], 1)
                        else:
                            pm.then_inc(pv_done, 1)
                    elif kind == "mx":
                        _, b, qb, h, half = st
                        if b == 0 and (qb, h, half) == (0, 0, 0):
                            pe.wait_ge(stack_dma, STACK_LOADS * nth[("qk", b)])
                        c0, cn = HALVES[half]
                        mm = pe.matmul(T[0:BLK, 0:cn], QS[0:SHIFT_ROW, b, h, qb * BLK:(qb + 1) * BLK],
                                       KS[0:SHIFT_ROW, b, h, c0:c0 + cn], start=True, stop=True)
                    elif kind == "mrow":
                        pe.wait_ge(nm_ready, (nth[st] + 1) // 2)
                        for k in range(4) if st[2] == 0 else range(3):
                            qb = k + 4 * st[2]
                            mm = pe.transpose(T[0:HEADS, k * BLK:(k + 1) * BLK],
                                              NMM[:, qb * HEADS:(qb + 1) * HEADS], ident[0:BLK, 0:BLK])
                    elif kind == "embed":
                        half = st[1]
                        pe.wait_ge(x_dma, X_LOADS * (half + 1))
                        for px in range(PATCH):
                            rhs = X[:, :, :].rearrange("p i (j q) -> p i j q", q=PATCH)[:, :, :, px]
                            mm = pe.matmul(T[:, 0:GHALF], w("emb", px, 128)[0:96, :], rhs,
                                           start=px == 0, stop=px == PATCH - 1)
                    elif kind == "gw":
                        _, layer, half = st
                        if half == 0:
                            if layer < 3:
                                pe.wait_ge(ht_scaled, 2 * layer + 2)
                            else:
                                pe.wait_ge(ht_relu, 6)
                        size = GBLK if layer < 3 else BLK
                        rhs = w("gcn", layer, 128) if layer < 3 else w("out")
                        for k in range(4) if half == 0 else range(3):
                            at = (k + 4 * half) * size
                            m = min(size, PATCHES - at)
                            mm = pe.matmul(T[0:m, k * 128:(k + 1) * 128], HT[:, at:at + m], rhs, start=True, stop=True)
                    elif kind == "gagg":
                        _, layer, half = st
                        if half == 0:
                            for g in ("gw", layer, 0), ("gw", layer, 1):
                                read(pe, turn, g)
                        for k in range(NG):
                            for part in (UH, UL):
                                mm = pe.matmul(T[:, 0:GHALF], part[:, k, :], adj[:, k, half * GHALF:(half + 1) * GHALF],
                                               start=k == 0 and part is UH, stop=k == NG - 1 and part is UL)
                    elif kind == "xt":
                        lnk = nth[("ln", st[1], st[2])]
                        pe.wait_ge(normed, lnk)
                        for k in range(NB):
                            t, at = (0, k) if k < 4 else (1, k - 4)
                            src = XN[st[2]][:, k, :, :].rearrange("p a f -> p (a f)")
                            mm = pe.transpose(T[:, t, at * BLK:(at + 1) * BLK], src, ident[0:BLK, 0:BLK])
                    elif kind in ("qk", "l1"):
                        b = st[1]
                        xs = XS["a" if kind == "qk" else "m"]
                        read(pe, turn, ("xt", b, "a" if kind == "qk" else "m"))
                        name, e, cols = ("qk", 0, 128) if kind == "qk" else \
                            (("eW1", st[2], 128) if st[2] < EXPERTS else ("sW1", 0, 128))
                        for part in (WH, WL):
                            for t, (c0, cn) in enumerate(HALVES):
                                mm = pe.matmul(T[:, t, 0:cn], wsplit(part, name, e, cols), xs[:, c0:c0 + cn],
                                               start=part is WH, stop=part is WL, skip_group_check=True)
                    elif kind in ("v", "gate"):
                        b = st[1]
                        xs = XS["a" if kind == "v" else "m"]
                        read(pe, turn, ("xt", b, "a" if kind == "v" else "m"))
                        cols = HID if kind == "v" else EXPERTS
                        for k in range(NB):
                            for part in (WH, WL):
                                mm = pe.matmul(T[0:BLK, 0, k * cols:(k + 1) * cols], xs[:, k * BLK:(k + 1) * BLK],
                                               wsplit(part, "v" if kind == "v" else "gW"),
                                               start=part is WH, stop=part is WL)
                    elif kind == "ot":
                        read(pe, turn, ("pv", st[1], 0, 0))
                        for k in range(4) if st[2] == 0 else range(3):
                            at = (k + 4 * st[2]) * BLK
                            mm = pe.transpose(T[0:BLK, k * 128:(k + 1) * 128], OT[:, at:at + BLK], ident[:, :])
                    elif kind == "obt":
                        for part in range(2):
                            read(pe, turn, ("ot", st[1], part))
                        for k in range(NB):
                            mm = pe.transpose(ps_bf[0:64, k * (BLK + 1):k * (BLK + 1) + BLK],
                                              OB[:, k, :, :].rearrange("p h d -> p (h d)"), ident_bf[0:BLK, 0:BLK])
                    elif kind == "wo":
                        read(pe, turn, ("obt", st[1]))
                        for k in range(NB):
                            for part in range(3):
                                mm = pe.matmul(T[0:BLK, k * HID:(k + 1) * HID], OBT[:, k, 0:BLK], wo3[:, part, :],
                                               start=part == 0, stop=part == 2)
                    elif kind == "l2":
                        _, b, j = st
                        for e in ((2 * j, 2 * j + 1) if j < 2 else (4,)):
                            read(pe, turn, ("l1", b, e))
                        for t, (c0, cn) in enumerate(PIECES):
                            if j == 2:
                                mm = pe.matmul(T[:, t, 0:cn], w("sW2"), H1[4][:, c0:c0 + cn], start=True, stop=True)
                                continue
                            for g in range(2):
                                e = 2 * j + g
                                mm = pe.matmul(T[64 * g:64 * g + 64, t, 0:cn], w("eW2", e, 64), H1[e][:, c0:c0 + cn],
                                               start=True, stop=True, tile_position=(0, 64 * g))
                    elif kind == "wb":
                        _, b, j = st
                        pe.wait_ge(g_wide, nth[("g3", b)])
                        for k in range(NB):
                            t, at = (0, k) if k < 4 else (1, k - 4)
                            src = GWW[:, k, 2 * j:2 * j + 2, :].rearrange("p a f -> p (a f)")
                            mm = pe.transpose(T[:, t, at * BLK:(at + 1) * BLK], src, ident[0:BLK, 0:BLK])
                    elif kind == "l3":
                        b = st[1]
                        for s_ in (("wb", b, 0), ("wb", b, 1), ("l2", b, 2)):
                            read(pe, turn, s_)
                        for j in range(3):
                            lhs = w("eW3", j, 64) if j < 2 else w("sW3")
                            for t, (c0, cn) in enumerate(PIECES):
                                mm = pe.matmul(T[64 * t:64 * t + 64, 0, 0:cn], lhs, H2[j][:, c0:c0 + cn],
                                               start=j == 0, stop=j == 2, tile_position=(0, 64 * t))
                    elif kind == "back":
                        read(pe, turn, ("l3", st[1]))
                        for k in range(NB):
                            t, at = (0, k) if k < 4 else (1, k - 4)
                            mm = pe.transpose(T[0:BLK, t, at * HID:(at + 1) * HID],
                                              OT2[64 * t:64 * t + 64, at * BLK:(at + 1) * BLK],
                                              ident[64 * t:64 * t + 64, 64 * t:64 * t + 64])
                    if mm is not None:
                        mm.then_inc(full[r], 1)

            rounds(pe, run, report(pe))


def _stack(*a):
    return np.concatenate(a, axis=0)


def _side(*a):
    return np.concatenate(a, axis=1)


def _diag(m):
    z = np.zeros_like(m)
    return _stack(_side(m, z), _side(z, m))


def _pad(m):
    return _stack(m, np.zeros((128 - m.shape[0], m.shape[1]), m.dtype))


def _twice(m):
    return _stack(m, m)


def _col(b):
    return np.reshape(b, (-1, 1))


def constants():
    ident = np.eye(128, dtype=np.float32)
    pos = np.arange(PATCHES, dtype=np.float32)[:, None]
    div = np.exp(np.arange(0, HID, 2, dtype=np.float32) * np.float32(-np.log(10000.0) / HID)).astype(np.float32)
    pe = np.zeros((PATCHES, HID), np.float32)
    pe[:, 0::2] = np.sin(pos * div)
    pe[:, 1::2] = np.cos(pos * div)
    iota = np.broadcast_to(np.arange(PATCHES, dtype=np.float32), (128, PATCHES))
    before = np.tril(np.ones((EXPERTS, EXPERTS), np.float32), -1).reshape(1, -1)
    return np.ascontiguousarray(_side(ident, _twice(pe.T), iota, np.broadcast_to(before, (128, 16))))


def layout(i):
    i = {k: np.asarray(v) for k, v in i.items()}
    t, a, f = "L0_tok_", "L0_attn_", "L0_ffn_"
    we = i[t + "W_embed"].reshape(CH * PATCH, PATCH, HID)
    emb = _side(*[_pad(_diag(we[:, px, :])) for px in range(PATCH)])
    gcn = _side(*[_diag(i[t + "W_gcn"][n]) for n in range(3)])
    plain = _side(emb, gcn, _diag(i[t + "W_out"]), _pad(i[a + "Wo"].T),
                  *[i[f + "eW2"][e] for e in range(EXPERTS)], _pad(i[f + "sW2"]),
                  _stack(i[f + "eW3"][0], i[f + "eW3"][1]), _stack(i[f + "eW3"][2], i[f + "eW3"][3]), i[f + "sW3"],
                  _col(_twice(i[t + "b_embed"])), *[_col(_twice(i[t + "b_gcn"][n])) for n in range(3)],
                  _col(_stack(i[a + "bq"], i[a + "bk"])), *[_col(i[f + "eb1"][e]) for e in range(EXPERTS)],
                  _col(_twice(i[f + "sb1"])), _col(_stack(i[f + "eb2"][0], i[f + "eb2"][1])),
                  _col(_stack(i[f + "eb2"][2], i[f + "eb2"][3])), _col(i[f + "sb2"]))
    split = _twice(_side(i[a + "Wq"].T, i[a + "Wk"].T, i[a + "Wv"].T, *[i[f + "eW1"][e] for e in range(EXPERTS)],
                         i[f + "sW1"], i[f + "sW1"], i[f + "gW"]))
    rows = np.concatenate([i[t + "b_out"], i[a + "bv"], i[a + "bo"], i[f + "gb"], i[f + "sb3"],
                           i[f + "eb3"].reshape(-1)]).reshape(1, -1)
    return {"x": i["x"], "txt": i["txt"], "edges": i[t + "edge_index"], "plain": plain, "split": split,
            "rows": rows, "const": constants()}


def kernel(**inputs):
    import concourse.bacc as bacc
    from concourse.bass_utils import run_bass_kernel_spmd

    nc = bacc.Bacc("TRN2", target_bir_lowering=False, num_devices=1)
    arrays = {f"in_{k}": np.ascontiguousarray(v) for k, v in layout(inputs).items()}
    args = [nc.dram_tensor(k, v.shape, mybir.dt.from_np(v.dtype), kind="ExternalInput").ap() for k, v in arrays.items()]
    batch = arrays["in_x"].shape[0]
    out = nc.dram_tensor("out_0", (batch, TOKENS, HID), F32, kind="ExternalOutput").ap()
    build(nc, batch // 2, *args, out)
    r = run_bass_kernel_spmd(nc, [arrays], core_ids=[0])
    return r.results[0]["out_0"]
```

```python
from contextlib import ExitStack

import concourse.bass as bass
import numpy as np
from concourse import mybir

F32 = mybir.dt.float32
F32R = mybir.dt.float32r
BF16 = mybir.dt.bfloat16
I32 = mybir.dt.int32
ALU = mybir.AluOpType
ACT = mybir.ActivationFunctionType
AX = mybir.AxisListType

GRID, PATCH, CH, HID = 28, 8, 3, 64
PATCHES = GRID * GRID
TEXT = 77
TOKENS = PATCHES + TEXT
BLK = 123
NB = TOKENS // BLK
GBLK = 112
NG = PATCHES // GBLK
GHALF = PATCHES // 2
HEADS, HD = 4, 16
SCALE = HD ** -0.5
EXPERTS = 4
EPS = 1e-5
STACK_LOADS = 8 * 16
X_LOADS = 2 * CH * 16
EDGES = 2 * 2 * GRID * (GRID - 1)
ECH = 126
NEC = EDGES // ECH
SHIFT_ROW = 96
HW = 432
COLS = 2 * HW
HALVES = [(0, HW), (HW, HW)]
PIECES = [(0, 4 * BLK), (4 * BLK, 3 * BLK)]

def _columns(sizes):
    at, out = 0, {}
    for name, n in sizes:
        out[name] = (at, at + n)
        at += n
    return out, at


PLAIN, PLAIN_W = _columns([("emb", PATCH * 128), ("gcn", 3 * 128), ("out", 128), ("wo", 64),
                           ("eW2", EXPERTS * 64), ("sW2", 128), ("eW3", 2 * 64), ("sW3", 64),
                           ("b_emb", 1), ("b_gcn", 3), ("b_qk", 1), ("eb1", EXPERTS), ("sb1", 1),
                           ("eb2", 2), ("sb2", 1)])
SPLIT, SPLIT_W = _columns([("qk", 128), ("v", 64), ("eW1", EXPERTS * 128), ("sW1", 128), ("gW", EXPERTS)])
ROWS, ROWS_W = _columns([("b_out", 64), ("bv", 64), ("bo", 64), ("gb", EXPERTS), ("sb3", 64),
                         ("eb3", EXPERTS * 64)])
CONST, CONST_W = _columns([("ident", 128), ("pos", PATCHES), ("iota", PATCHES), ("before", 16)])


def graph_steps(*layers):
    out = []
    for layer in layers:
        out += [("embed", 0), ("embed", 1)] if layer == "e" else [("gw", layer, 0), ("gw", layer, 1)]
        out += [("wait", 2)] if layer == "e" else [("wait", 1)]
        out += [("gagg", layer, 0), ("gagg", layer, 1), ("wait", 2)] if layer in (0, 1, 2) else []
    return out


def norm_steps(b, which):
    return [(k, b, which) for k in ("ln", "ln2", "ln3")]


def stack_steps(b, which):
    return [("xt", b, which, 0), ("xt", b, which, 1), ("wait", 1)]


def max_steps(b):
    return [("mx", b, qb, h, half) for qb in range(NB) for h in range(HEADS) for half in range(2)] \
        + [("mrow", b, 0), ("mrow", b, 1)]


def attention_steps(b):
    units = [(kb, half, h) for kb in range(NB) for half in range(2) for h in range(HEADS)]
    out = []
    for n, (kb, half, h) in enumerate(units):
        out.append(("s", b, kb, half, h))
        if n >= HEADS + 1 and (n - 1) % HEADS == 0:
            kb, half, _ = units[n - 2]
            out.append(("pv", b, kb, half))
    return out + [("pv", b, NB - 1, 1)]


def finish_steps(b):
    return [("ot", b, 0), ("ot", b, 1), ("wait", 1), ("obt", b), ("wait", 1), ("wo", b)]


def expert_steps(b):
    out = [("gate", b)]
    for e in range(EXPERTS + 1):
        out += [("l1", b, e, 0), ("l1", b, e, 1)]
        out += {0: [("g2", b)], 1: [("g3", b)], 2: [("l2", b, 0, 0), ("l2", b, 0, 1), ("hb", b)], 3: [],
                4: [("l2", b, 1, 0), ("l2", b, 1, 1)]}[e]
    return out + [("wb", b, 0, 0), ("l2", b, 2, 0), ("wb", b, 0, 1), ("l2", b, 2, 1), ("wb", b, 1, 0), ("wb", b, 1, 1),
                  ("wait", 1), ("l3", b), ("wait", 1), ("back", b, 0), ("back", b, 1)]


def project_steps(b):
    return [("qk", b, 0), ("qk", b, 1), ("scratch", b)]


WAIT = 9
COST = {"s": 1, "pv": 4, "mx": 1, "embed": 34, "gw": 4, "gagg": 12, "xt": 4, "qk": 2, "v": 7, "gate": 7, "l1": 2,
        "l2": 4, "wb": 4, "l3": 25, "ot": 4, "obt": 2, "wo": 6, "back": 2, "mrow": 4}


def weave(*parts):
    placed = []
    for steps, start, end in parts:
        costs = [WAIT * st[1] if st[0] == "wait" else COST.get(st[0], 1) for st in steps]
        total, passed = sum(costs), 0
        for st, cost in zip(steps, costs):
            placed.append((start + (end - start) * passed / total, st))
            passed += cost
    return [st for _, st in sorted(placed, key=lambda p: p[0]) if st[0] != "wait"]


def round_steps(with_last, with_next):
    last = stack_steps(1, "m") + expert_steps(1) + [("hcopy", 1)] if with_last else [("hcopy", 1)]
    first = [(attention_steps(0), 0.0, 1.0), (max_steps(1), 0.3, 1.0)]
    if with_last:
        first += [(finish_steps(1), 0.0, 0.1), (norm_steps(1, "m"), 0.12, 0.2)]
        first += [(last, 0.22, 0.97)]
    else:
        first += [(last, 0.0, 0.0)]
    second = [(attention_steps(1), 0.02, 1.0), (finish_steps(0), 0.0, 0.12), (norm_steps(0, "m"), 0.14, 0.3)]
    experts = stack_steps(0, "m") + expert_steps(0)
    if with_next:
        first += [(graph_steps("e", 0, 1), 0.0, 1.0)]
        second += [(graph_steps(2, 3), 0.0, 0.25), (norm_steps(0, "a"), 0.26, 0.33), (norm_steps(1, "a"), 0.38, 0.5)]
        second += [(stack_steps(0, "a") + project_steps(0) + [("stack", 0), ("v", 0)], 0.34, 0.45)]
        second += [(stack_steps(1, "a") + project_steps(1), 0.55, 0.7)]
        second += [(max_steps(0), 0.6, 0.97)]
    second += [(experts, 0.31, 1.0)]
    return [("hcopy", 0), ("stack", 1), ("v", 1)] + weave(*first) + [("oev", 0)] + weave(*second) + [("oev", 1)]


def prologue_steps():
    return weave((graph_steps("e", 0, 1, 2, 3) + norm_steps(0, "a") + stack_steps(0, "a") + project_steps(0) \
        + [("stack", 0), ("v", 0)] + norm_steps(1, "a") + stack_steps(1, "a") + project_steps(1), 0, 1)) \
        + max_steps(0)


def epilogue_steps():
    return weave((finish_steps(1) + norm_steps(1, "m") + stack_steps(1, "m") + expert_steps(1), 0, 1))


ROTATING = ("s", "embed", "gw", "gagg", "mx", "mrow", "ot", "obt", "wo", "xt", "qk", "v", "gate", "l1", "l2", "wb", "l3",
          "back")


def turns(steps):
    held, count, out = {}, {}, {}
    turn = 0
    for st in steps:
        if st[0] in ROTATING:
            banks = ((0, 1, 2, 3, 6, 7)[turn % 6],)
            turn += 1
        elif st[0] == "pv" and st[2:] == (0, 0):
            banks = (4, 5)
        else:
            continue
        before = sorted({held[k] for k in banks if k in held})
        count[banks[0]] = count.get(banks[0], 0) + 1
        out[st] = (banks[0], count[banks[0]], before)
        for k in banks:
            held[k] = (banks[0], count[banks[0]])
    return out


def ordinal(steps):
    count, out = {}, {}
    for st in steps:
        count[st[0]] = count.get(st[0], 0) + 1
        out[st] = count[st[0]]
    return out


def build(nc, pairs, x, txt, edges, plain, split, rows, const, out):
    ctx = ExitStack()
    with ctx:
        def sb(name, shape, dt, where=ctx):
            return where.enter_context(nc.sbuf_tensor(name, shape, dt))

        def sem(name):
            return ctx.enter_context(nc.semaphore(name))

        ps = ctx.enter_context(nc.psum_tensor("ps", [128, 8, 512], F32))
        acc = ps[:, 4:6, :]

        W = sb("plain_w", [128, PLAIN_W], F32)
        WH = sb("split_hi", [128, SPLIT_W], F32R)
        WL = sb("split_lo", [128, SPLIT_W], F32R)
        RW = sb("bias_rows", [128, ROWS_W], F32)
        ident = sb("ident", [128, 128], F32)
        ident_bf = sb("ident_bf", [128, 128], BF16)
        before = sb("before", [128, 16], F32)
        wo3 = sb("wo_parts", [64, 3, 64], BF16)
        posb = sb("pos_and_bias", [128, PATCHES], F32)
        dinv = sb("dinv_row", [128, PATCHES], F32)
        adj = sb("adjacency", [GBLK, NG, PATCHES], F32R)

        def w(name, i=0, n=None):
            a, z = PLAIN[name]
            n = n or z - a
            return W[:, a + i * n:a + (i + 1) * n]

        def wsplit(tile, name, i=0, n=None):
            a, z = SPLIT[name]
            n = n or z - a
            return tile[:, a + i * n:a + (i + 1) * n]

        def row(name, i=0, n=64):
            a, _ = ROWS[name]
            return RW[0:BLK, a + i * n:a + (i + 1) * n]

        load_sem = sem("setup_load")
        const_sem = sem("setup_iota")
        init_v = sem("setup_vector")
        init_p = sem("setup_pool")
        hot_sem = sem("setup_onehot")
        cnt_full = sem("setup_counts_full")
        cnt_free = sem("setup_counts_free")
        deg_full = sem("setup_degree_full")
        root_sem = sem("setup_root")
        with ExitStack() as tmp:
            raw = sb("split_raw", [128, SPLIT_W], F32, tmp)
            iota = sb("iota", [128, PATCHES], F32, tmp)
            e_int = sb("edges_int", [ECH, 2, NEC], I32, tmp)
            e_f = sb("edges_f", [ECH, 2, NEC], F32, tmp)
            hot_s = sb("onehot_src", [ECH, NEC, PATCHES], BF16, tmp)
            hot_d = sb("onehot_dst", [ECH, NEC, PATCHES], BF16, tmp)
            ones = sb("ones", [ECH, 128], BF16, tmp)
            slide = sb("ident_slide", [GBLK, 2 * PATCHES + GBLK], BF16, tmp)
            deg = sb("degree", [128, PATCHES], F32, tmp)
            tmp1 = sb("newton", [128, PATCHES], F32, tmp)
            wor = sb("wo_rest", [64, 2, 64], F32, tmp)
            with nc.Block() as block:
                @block.sync
                def _(sp):
                    c = CONST
                    sp.dma_start(iota[:, :], const[:, c["iota"][0]:c["iota"][1]]).then_inc(const_sem, 16)
                    sp.dma_start(e_int[:, :, :], edges.rearrange("s (p c) -> p s c", p=ECH)
                                 ).then_inc(const_sem, 16)
                    sp.dma_start(W[:, :], plain).then_inc(load_sem, 16)
                    sp.dma_start(raw[:, :], split).then_inc(load_sem, 16)
                    sp.dma_start(RW[:, :], rows.to_broadcast([128, ROWS_W])).then_inc(load_sem, 16)
                    sp.dma_start(ident[:, :], const[:, c["ident"][0]:c["ident"][1]]).then_inc(load_sem, 16)
                    sp.dma_start(posb[:, :], const[:, c["pos"][0]:c["pos"][1]]).then_inc(load_sem, 16)
                    sp.dma_start(before[:, :], const[:, c["before"][0]:c["before"][1]]).then_inc(load_sem, 16)

                @block.gpsimd
                def _(pool):
                    pool.memset(ones[:, :], 1.0).then_inc(init_p, 1)
                    pool.memset(slide[:, :], 0.0).then_inc(init_p, 1)

                @block.vector
                def _(v):
                    done = [0]

                    def settle(ins):
                        done[0] += 1
                        ins.then_inc(init_v, 1)
                        v.wait_ge(init_v, done[0])

                    v.wait_ge(const_sem, 32)
                    settle(v.tensor_copy(e_f[:, :, :], e_int[:, :, :]))
                    for c in range(NEC):
                        v.tensor_scalar(hot_s[:, c, :], iota[0:ECH, :], e_f[:, 0, c:c + 1], None,
                                        ALU.is_equal).then_inc(hot_sem, 1)
                        v.tensor_scalar(hot_d[:, c, :], iota[0:ECH, :], e_f[:, 1, c:c + 1], None,
                                        ALU.is_equal).then_inc(hot_sem, 1)
                    v.wait_ge(load_sem, 96)
                    v.tensor_copy(ident_bf[:, :], ident[:, :])
                    v.wait_ge(init_p, 2)
                    settle(v.tensor_copy(slide[:, PATCHES:PATCHES + GBLK], ident[0:GBLK, 0:GBLK]))
                    settle(v.tensor_copy(WH[:, :], raw[:, :]))
                    v.tensor_tensor(WL[:, :], raw[:, :], WH[:, :].bitcast(F32), ALU.subtract)
                    settle(v.tensor_copy(wo3[:, 0, :], w("wo")[0:64, :]))
                    settle(v.tensor_tensor(wor[:, 0, :], w("wo")[0:64, :], wo3[:, 0, :], ALU.subtract))
                    settle(v.tensor_copy(wo3[:, 1, :], wor[:, 0, :]))
                    settle(v.tensor_tensor(wor[:, 1, :], wor[:, 0, :], wo3[:, 1, :], ALU.subtract))
                    v.tensor_copy(wo3[:, 2, :], wor[:, 1, :])
                    v.tensor_scalar(posb[:, :], posb[:, :], w("b_emb"), None, ALU.add)
                    v.wait_ge(deg_full, 1)
                    v.tensor_scalar(deg[:, :].rearrange("p (a n) -> p a n", a=2), ps[:, 6:8, 0:GHALF], 1.0, None,
                                    ALU.add).then_inc(root_sem, 1)
                    v.wait_ge(root_sem, 2)
                    settle(v.reciprocal(dinv[:, :], tmp1[:, :]))
                    settle(v.tensor_tensor(tmp1[:, :], dinv[:, :], dinv[:, :], ALU.mult))
                    settle(v.tensor_tensor(tmp1[:, :], tmp1[:, :], deg[:, :], ALU.mult))
                    settle(v.tensor_scalar(tmp1[:, :], tmp1[:, :], -0.5, 1.5, ALU.mult, ALU.add))
                    settle(v.tensor_tensor(dinv[:, :], dinv[:, :], tmp1[:, :], ALU.mult))

                @block.scalar
                def _(a):
                    a.wait_ge(root_sem, 1)
                    a.activation(tmp1[:, :], deg[:, :], ACT.Sqrt).then_inc(root_sem, 1)
                    for n in range(2 * NG):
                        half, sblk = n // NG, n % NG
                        a.wait_ge(cnt_full, n + 1)
                        a.activation(adj[:, sblk, half * GHALF:(half + 1) * GHALF], ps[0:GBLK, n % 6, 0:GHALF],
                                     ACT.Copy).then_inc(cnt_free, 1)

                @block.tensor
                def _(pe):
                    pe.wait_ge(hot_sem, 2 * NEC)
                    pe.wait_ge(init_p, 2)
                    for c in range(NEC):
                        for half in range(2):
                            mm = pe.matmul(ps[:, 6 + half, 0:GHALF], ones[:, :],
                                           hot_d[:, c, half * GHALF:(half + 1) * GHALF],
                                           start=c == 0, stop=c == NEC - 1)
                    mm.then_inc(deg_full, 1)
                    pe.wait_ge(init_v, 2)
                    for n in range(2 * NG):
                        half, sblk = n // NG, n % NG
                        if n >= 6:
                            pe.wait_ge(cnt_free, n - 5)
                        at = PATCHES - sblk * GBLK + half * GHALF
                        pe.matmul(ps[0:GBLK, n % 6, 0:GHALF], slide[:, PATCHES:PATCHES + GBLK],
                                  slide[:, at:at + GHALF], start=True, stop=False)
                        for c in range(NEC):
                            mm = pe.matmul(ps[0:GBLK, n % 6, 0:GHALF], hot_s[:, c, sblk * GBLK:(sblk + 1) * GBLK],
                                           hot_d[:, c, half * GHALF:(half + 1) * GHALF],
                                           start=False, stop=c == NEC - 1)
                        mm.then_inc(cnt_full, 1)

        xm = sb("image_rows", [128, GRID // 2 * GRID * PATCH], F32)
        X = xm[0:96, :].rearrange("p (i w) -> p i w", i=GRID // 2)
        MR = xm[96:96 + HEADS, 0:COLS].bitcast(F32R)
        HT = sb("nodes_T", [128, PATCHES], F32)
        parts = [sb(n, [128, NG * 128], F32R) for n in ("parts_hi", "parts_lo")]
        UH, UL = (p[0:GBLK, :].rearrange("p (k n) -> p k n", n=128) for p in parts)
        QKH, QKL = (p[:, 0:COLS] for p in parts)
        HN = sb("tokens_next", [BLK, NB, 2, HID], F32)
        H = sb("tokens", [BLK, NB, 2, HID], F32)
        XC = sb("centred", [BLK, NB, HID], F32)
        SQ = sb("squared", [BLK, NB, HID], F32)
        XN = {k: sb(f"normed_twice_{k}", [BLK, NB, 2, HID], F32) for k in "am"}
        st7 = sb("ln_stats", [BLK, 4, NB], F32)
        halfneg = sb("minus_half", [BLK, NB], F32)
        XS = {"a": sb("x_stack_attn", [128, COLS], F32R), "m": sb("x_stack_moe", [128, COLS], F32R)}
        QS = sb("q_stack", [SHIFT_ROW + 1, 2, HEADS, COLS], F32R)
        KS = sb("k_stack", [SHIFT_ROW + 1, 2, HEADS, COLS], F32R)
        VV = sb("v_and_one", [BLK, 2, NB, HEADS, 32], F32)
        P = sb("probs", [BLK, 2, HEADS, HW], F32)
        H1 = [sb(f"hidden1_{n}", [128, COLS], F32) for n in range(3)]
        H2 = [sb(f"hidden2_{n}", [128, TOKENS], F32) for n in range(3)]
        NM = sb("neg_max_halves", [BLK, NB * HEADS, 2], F32)
        NMM = sb("neg_max", [BLK, NB * HEADS], F32)
        OT = sb("attn_T", [128, COLS], F32)
        RC = sb("inv_sums", [BLK, NB, HEADS], F32)
        OB = sb("attn_bf", [BLK, NB, HEADS, HD], BF16)
        OBT = sb("attn_bf_T", [64, NB, BLK + 1], BF16)
        OT2 = sb("moe_T", [128, 4 * BLK], F32)
        GZ = sb("gate_vals", [BLK, 4, NB, EXPERTS], F32)
        GS = sb("gate_sums", [BLK, 2, NB], F32)
        GC = sb("gate_cmp", [BLK, 2, NB, EXPERTS, EXPERTS], F32)
        GW = sb("gate_weights", [BLK, NB, EXPERTS], F32)
        GWW = sb("gate_weights_wide", [BLK, NB, EXPERTS, HID], F32)
        TMP = OT2[0:BLK, 0:NB * HID].rearrange("p (k f) -> p k f", f=HID)
        OUTT = sb("out_tile", [BLK, NB, HID], F32)

        def blocks_of(t):
            return [(k, k) for k in range(4)] if t == 0 else [(k, k - 4) for k in range(4, NB)]

        def halves(ap):
            return ap.rearrange("p (t n) -> p t n", t=2)

        scratch = nc.dram_tensor("qk_scratch", (2, 2, 2, HEADS, HD, COLS), F32, kind="Internal").ap()

        full = {r: sem(f"bank{r}_full") for r in range(8)}
        free = {r: sem(f"bank{r}_free") for r in range(8)}
        x_dma, txt_dma = sem("x_dma"), sem("txt_dma")
        hcopied = sem("tokens_copied")
        ht_scaled, ht_relu = sem("ht_scaled"), sem("ht_relu")
        centred, squared, var_ready, rstd_ready, normed = (sem(n) for n in
                                                           ("centred_s", "squared_s", "var_ready", "rstd_ready", "normed_s"))
        xt_hi, qk_hi, stack_dma, nm_ready, mrow_dma = (
            sem(n) for n in ("xt_hi", "qk_hi_s", "stack_dma", "nm_ready", "mrow_dma"))
        pv_done = sem("pv_done")
        g_sub, g_exp, g_prob, g_exp2, g_weight, hb_ready = (
            sem(n) for n in ("g_sub", "g_exp", "g_prob", "g_exp2", "g_weight", "hb_ready"))
        out_dma, g_wide, scratch_dma = sem("out_dma"), sem("g_wide"), sem("scratch_dma")
        v_chain, p_chain = sem("v_chain"), sem("p_chain")
        round_sems = [*full.values(), *free.values(), x_dma, txt_dma, hcopied, ht_scaled, ht_relu, centred, squared,
                      var_ready, rstd_ready, normed, xt_hi, qk_hi, stack_dma, nm_ready, mrow_dma, pv_done, g_sub,
                      g_exp, g_prob, g_exp2, g_weight, hb_ready, out_dma, g_wide, scratch_dma, v_chain, p_chain]
        arrived = sem("arrived")
        numbers = [s.num for s in (*round_sems, arrived)]
        assert sorted(numbers) == list(range(min(numbers), max(numbers) + 1))
        go = sem("go")

        def read(eng, turn, st):
            r, n, _ = turn[st]
            eng.wait_ge(free[r], n)

        def rounds(eng, run, end):
            run(prologue_steps(), None)
            end(1)
            if pairs > 1:
                run(round_steps(False, True), 0)
                end(2)
            if pairs > 2:
                middle = round_steps(True, True)
                with eng.Fori(1, pairs - 1) as i:
                    run(middle, i)
                    end(i + 2)
            run(round_steps(pairs > 1, False), pairs - 1)
            end(pairs + 1)
            run(epilogue_steps(), pairs)

        def report(eng):
            def end(n):
                eng.drain().then_inc(arrived, 1)
                eng.wait_ge(go, n)
                if isinstance(n, int):
                    eng.drain()
            return end

        block = ctx.enter_context(nc.Block())

        @block.sync
        def _(sp):
            def run(steps, i):
                turn, nth = turns(steps), ordinal(steps)
                has_next = ("embed", 0) in turn
                nxt = 0 if i is None else i + 1
                if i is None:
                    sp.wait_ge(v_chain, 1)
                if i is None:
                    load_text(nxt)
                if has_next:
                    load_rows(nxt, 0)
                for st in steps:
                    kind = st[0]
                    if kind == "hcopy":
                        if has_next and nth[st] == 2:
                            sp.wait_ge(hcopied, 2)
                            load_text(nxt)
                    elif kind == "embed" and st[1] == 0:
                        r, n, _ = turn[st]
                        sp.wait_ge(full[r], n)
                        load_rows(nxt, 1)
                    elif kind == "scratch":
                        b = st[1]
                        sp.wait_ge(qk_hi, 2 * (b + 1))
                        read(sp, turn, ("qk", b, 0))
                        read(sp, turn, ("qk", b, 1))
                        for part, tile in enumerate((QKH, QKL)):
                            sp.dma_start(scratch[b, part].rearrange("a h r c -> (a h r) c"), tile.bitcast(F32)
                                         ).then_inc(scratch_dma, 16)
                    elif kind == "stack":
                        b = st[1]
                        if b == 0:
                            sp.wait_ge(scratch_dma, 32)
                        for part in range(2):
                            q_part = scratch[b, part, 0].rearrange("h r c -> r h c")
                            k_part = scratch[b, part, 1].rearrange("h r c -> r h c")
                            for copy in range(2):
                                rq, rk = HD * (2 * copy + part), HD * (2 * part + copy)
                                sp.dma_start(QS[rq:rq + HD, b, :, :].bitcast(F32), q_part).then_inc(stack_dma, 16)
                                sp.dma_start(KS[rk:rk + HD, b, :, :].bitcast(F32), k_part).then_inc(stack_dma, 16)
                    elif kind == "mrow" and st[2] == 1:
                        read(sp, turn, ("mrow", st[1], 0))
                        read(sp, turn, st)
                        for h in range(HEADS):
                            sp.dma_start(QS[SHIFT_ROW:SHIFT_ROW + 1, st[1], h, :].bitcast(F32), MR[h:h + 1, :].bitcast(F32)
                                         ).then_inc(mrow_dma, 16)
                    elif kind == "back" and st[2] == 1:
                        read(sp, turn, ("back", st[1], 0))
                        read(sp, turn, st)
                        image = i * 2 if st[1] == 0 else (i - 1) * 2 + 1
                        dst = out[bass.ds(image, 1), :, :].rearrange("o (n p) f -> (o p) n f", p=BLK)
                        sp.dma_start(dst, OUTT[:, :, :]).then_inc(out_dma, 16)
                def landed(semaphore, count):
                    if count:
                        sp.wait_ge(semaphore, count)

                landed(x_dma, 2 * X_LOADS * has_next)
                landed(txt_dma, 32 * has_next)
                landed(out_dma, 16 * sum(st[0] == "l3" for st in steps))
                landed(scratch_dma, 32 * sum(st[0] == "scratch" for st in steps))
                landed(stack_dma, STACK_LOADS * sum(st[0] == "stack" for st in steps))
                landed(mrow_dma, 64 * sum(st[0] == "mrow" for st in steps) // 2)

            def load_text(nxt):
                for b in range(2):
                    sp.dma_start(HN[PATCHES - 6 * BLK:BLK, NB - 1, b, :],
                                 txt[bass.ds(nxt * 2 + b, 1), :, :].rearrange("o t f -> (o t) f")
                                 ).then_inc(txt_dma, 16)

            def load_rows(nxt, half):
                rows = GRID * PATCH // 2
                for b in range(2):
                    for c in range(CH):
                        src = x[bass.ds(nxt * 2 + b, 1), c, half * rows:(half + 1) * rows, :]
                        p = (b * CH + c) * PATCH
                        sp.dma_start(X[p:p + PATCH, :, :], src.rearrange("o (i q) w -> (o q) i w", q=PATCH)
                                     ).then_inc(x_dma, 16)

            def end(n):
                sp.wait_ge(arrived, 4)
                sp.sem_clear(range(min(numbers), max(numbers) + 1))
                sp.drain().then_inc(go, 1)

            rounds(sp, run, end)

        @block.gpsimd
        def _(pool):
            chain = [0]

            def settle(ins):
                chain[0] += 1
                ins.then_inc(p_chain, 1)
                pool.wait_ge(p_chain, chain[0])

            def run(steps, i):
                chain[0] = 0
                turn, nth = turns(steps), ordinal(steps)
                if i is None:
                    settle(pool.memset(halfneg[:, :], -0.5))
                    for tile in (XS["a"], XS["m"], MR):
                        settle(pool.memset(tile[:, TOKENS:COLS].bitcast(F32), 0.0))
                    settle(pool.memset(VV[:, :, :, :, :], 0.0))
                    settle(pool.memset(VV[:, :, :, :, HD:HD + 1], 1.0))
                    settle(pool.memset(QS[64:SHIFT_ROW, :, :, :].bitcast(F32), 0.0))
                    settle(pool.memset(KS[64:SHIFT_ROW, :, :, :].bitcast(F32), 0.0))
                    settle(pool.memset(KS[SHIFT_ROW:SHIFT_ROW + 1, :, :, :].bitcast(F32), 1.0))
                for st in steps:
                    kind = st[0]
                    if kind == "hcopy":
                        b = st[1]
                        if b == 1 and ("back", b, 1) in turn:
                            for t in range(2):
                                read(pool, turn, ("back", b, t))
                        pool.tensor_copy(H[:, :, b, :], HN[:, :, b, :]).then_inc(hcopied, 1)
                    elif kind == "embed":
                        c = slice(st[1] * GHALF, (st[1] + 1) * GHALF)
                        read(pool, turn, st)
                        pool.tensor_tensor(HT[:, c], HT[:, c], dinv[:, c], ALU.mult).then_inc(ht_scaled, 1)
                    elif kind == "gagg" and st[1] < 2:
                        c = slice(st[2] * GHALF, (st[2] + 1) * GHALF)
                        pool.wait_ge(ht_relu, nth[st])
                        pool.tensor_tensor(HT[:, c], HT[:, c], dinv[:, c], ALU.mult).then_inc(ht_scaled, 1)
                    elif kind == "ln2":
                        n = nth[st]
                        pool.wait_ge(var_ready, n)
                        pool.tensor_tensor(st7[:, 3, :], st7[:, 2, :], halfneg[:, :], ALU.pow).then_inc(rstd_ready, 1)
                    elif kind == "hb":
                        b = st[1]
                        pool.wait_ge(g_weight, nth[st])
                        hb = H[:, :, b, :]
                        shape = [BLK, NB, HID]
                        settle(pool.tensor_tensor(hb, hb, row("sb3").unsqueeze(1).to_broadcast(shape), ALU.add))
                        for e in range(EXPERTS):
                            settle(pool.tensor_tensor(TMP[:, :, :], GW[:, :, e:e + 1].to_broadcast(shape),
                                                      row("eb3", e).unsqueeze(1).to_broadcast(shape), ALU.mult))
                            ins = pool.tensor_tensor(hb, hb, TMP[:, :, :], ALU.add)
                            if e < EXPERTS - 1:
                                settle(ins)
                        ins.then_inc(hb_ready, 1)

            rounds(pool, run, report(pool))

        @block.scalar
        def _(act):
            def run(steps, i):
                turn, nth = turns(steps), ordinal(steps)
                for st in steps:
                    kind = st[0]
                    r, n, prior = turn.get(st, (None, 0, ()))
                    if r is not None:
                        T = ps[:, r, :]
                    if kind == "s":
                        _, b, kb, half, h = st
                        act.wait_ge(full[r], n)
                        if h == 0 and kb >= 1:
                            act.wait_ge(pv_done, b * (2 * NB - 1) + 2 * (kb - 1) + half + 1)
                        elif h == 0 and b == 1:
                            act.wait_ge(full[4], turn[("pv", 0, 0, 0)][1])
                        act.activation(P[:, half, h, :], T[0:BLK, 0:HW], ACT.Exp,
                                       scale=SCALE).then_inc(free[r], 1)
                    elif kind == "gw" and st[1] < 3:
                        half = st[2]
                        blocks = range(4) if half == 0 else range(4, NG)
                        act.wait_ge(full[r], n)
                        act.activation(UH[:, blocks[0]:blocks[-1] + 1, :].rearrange("p k n -> p (k n)"),
                                       T[0:GBLK, 0:128 * len(blocks)], ACT.Copy).then_inc(xt_hi, 1)
                    elif kind == "gagg":
                        c = slice(st[2] * GHALF, (st[2] + 1) * GHALF)
                        read(act, turn, st)
                        act.activation(HT[:, c], HT[:, c], ACT.Relu, bias=w("b_gcn", st[1], 1)).then_inc(ht_relu, 1)
                    elif kind == "xt":
                        act.wait_ge(full[r], n)
                        c0, cn = PIECES[st[3]]
                        act.activation(XS[st[2]][:, c0:c0 + cn], T[:, 0:cn], ACT.Copy).then_inc(xt_hi, 1)
                    elif kind == "qk":
                        c0, cn = HALVES[st[2]]
                        act.wait_ge(full[r], n)
                        if st[1:] == (1, 0):
                            act.wait_ge(scratch_dma, 32)
                        act.activation(QKH[:, c0:c0 + cn], T[:, 0:cn], ACT.Identity, bias=w("b_qk")).then_inc(qk_hi, 1)
                    elif kind == "mrow":
                        c0, cn = PIECES[st[2]]
                        act.wait_ge(full[r], n)
                        if nth[st] > 2:
                            act.wait_ge(mrow_dma, 64 * ((nth[st] - 1) // 2))
                        act.activation(MR[:, c0:c0 + cn], T[0:HEADS, 0:cn], ACT.Copy).then_inc(free[r], 1)
                    elif kind == "oev":
                        rv, nv, _ = turn[("pv", st[1], 0, 0)]
                        act.wait_ge(full[rv], nv)
                        act.activation(halves(OT[:, :]), acc[:, :, 0:HW], ACT.Copy).then_inc(free[rv], 1)
                    elif kind == "obt":
                        act.wait_ge(full[r], n)
                        act.activation(OBT[:, :, 0:BLK],
                                       T.bitcast(BF16)[0:64, 0:NB * (BLK + 1)].rearrange("p (k n) -> p k n", k=NB)[:, :, 0:BLK],
                                       ACT.Copy).then_inc(free[r], 1)
                    elif kind == "ln":
                        act.wait_ge(centred, nth[st])
                        act.activation(SQ[:, :, :], XC[:, :, :], ACT.Square).then_inc(squared, 1)
                    elif kind == "g3":
                        act.wait_ge(g_weight, nth[st])
                        act.activation(GWW[:, :, :, :], GW[:, :, :].unsqueeze(3).to_broadcast([BLK, NB, EXPERTS, HID]),
                                       ACT.Copy).then_inc(g_wide, 1)
                    elif kind == "gate":
                        act.wait_ge(g_sub, nth[st])
                        act.activation(GZ[:, 1, :, :], GZ[:, 0, :, :], ACT.Exp).then_inc(g_exp, 1)
                    elif kind == "g2":
                        act.wait_ge(g_prob, nth[st])
                        act.activation(GZ[:, 3, :, :], GZ[:, 2, :, :], ACT.Exp).then_inc(g_exp2, 1)
                    elif kind == "l1":
                        e = st[2]
                        bias = w("eb1", e, 1) if e < EXPERTS else w("sb1")
                        act.wait_ge(full[r], n)
                        c0, cn = HALVES[st[3]]
                        act.activation(H1[e % 3][:, c0:c0 + cn], T[:, 0:cn], ACT.Relu, bias=bias).then_inc(free[r], 1)
                    elif kind == "l2":
                        j = st[2]
                        bias = w("eb2", j, 1) if j < 2 else w("sb2")
                        c0, cn = PIECES[st[3]]
                        act.wait_ge(full[r], n)
                        act.activation(H2[j][:, c0:c0 + cn], T[:, 0:cn], ACT.Relu, bias=bias).then_inc(free[r], 1)
                    elif kind == "l3":
                        act.wait_ge(full[r], n)
                        act.wait_ge(hb_ready, nth[st])
                        act.activation(OT2[0:64, 0:4 * BLK], T[0:64, 0:4 * BLK], ACT.Copy)
                        act.activation(OT2[64:128, 0:3 * BLK], T[64:128, 0:3 * BLK], ACT.Copy).then_inc(free[r], 1)

            rounds(act, run, report(act))

        @block.vector
        def _(v):
            chain = [0]

            def settle(ins):
                chain[0] += 1
                ins.then_inc(v_chain, 1)
                v.wait_ge(v_chain, chain[0])

            def run(steps, i):
                chain[0] = 0
                turn, nth = turns(steps), ordinal(steps)
                if i is None:
                    settle(v.memset(X[:, :, :], 0.0))
                    v.wait_ge(p_chain, 9)
                hi_no = {}
                for st in steps:
                    if st[0] == "xt" or (st[0] == "gw" and st[1] < 3):
                        hi_no[st] = len(hi_no) + 1
                for st in steps:
                    kind = st[0]
                    r, n, prior = turn.get(st, (None, 0, ()))
                    if r is not None:
                        T = ps[:, r, :]
                    if kind == "mx":
                        _, b, qb, h, half = st
                        v.wait_ge(full[r], n)
                        keys = min(HW, TOKENS - half * HW)
                        v.tensor_reduce(NM[:, qb * HEADS + h, half:half + 1], T[0:BLK, 0:keys], AX.X, ALU.max,
                                        negate=True).then_inc(free[r], 1)
                        if (qb, h, half) == (NB - 1, HEADS - 1, 1):
                            v.wait_ge(free[r], n)
                            v.tensor_reduce(NMM[:, :], NM[:, :, :], AX.X, ALU.min).then_inc(nm_ready, 1)
                    elif kind == "embed":
                        c = slice(st[1] * GHALF, (st[1] + 1) * GHALF)
                        v.wait_ge(full[r], n)
                        v.tensor_tensor(HT[:, c], T[:, 0:GHALF], posb[:, c], ALU.add).then_inc(free[r], 1)
                    elif kind == "gw" and st[1] < 3:
                        half = st[2]
                        blocks = range(4) if half == 0 else range(4, NG)
                        k = slice(blocks[0], blocks[-1] + 1)
                        v.wait_ge(xt_hi, hi_no[st])
                        v.tensor_tensor(UL[:, k, :], T[0:GBLK, 0:128 * len(blocks)].rearrange("p (k n) -> p k n", n=128),
                                        UH[:, k, :].bitcast(F32), ALU.subtract).then_inc(free[r], 1)
                    elif kind == "gw":
                        v.wait_ge(full[r], n)
                        if i is not None:
                            v.wait_ge(hcopied, 2)
                        bias = row("b_out")
                        jobs = [(0, 4, BLK)] if st[2] == 0 else [(4, 2, BLK), (6, 1, PATCHES - 6 * BLK)]
                        for k0, kn, np_ in jobs:
                            o = (k0 - 4 * st[2]) * 128
                            ins = v.tensor_tensor(
                                HN[0:np_, k0:k0 + kn, :, :].rearrange("p k b f -> p (k b) f"),
                                T[0:np_, o:o + kn * 128].rearrange("p (k f) -> p k f", f=HID),
                                bias[0:np_, :].unsqueeze(1).to_broadcast([np_, kn * 2, HID]), ALU.add)
                        ins.then_inc(free[r], 1)
                    elif kind == "gagg":
                        c = slice(st[2] * GHALF, (st[2] + 1) * GHALF)
                        v.wait_ge(full[r], n)
                        v.tensor_tensor(HT[:, c], T[:, 0:GHALF], dinv[:, c], ALU.mult).then_inc(free[r], 1)
                    elif kind == "ln":
                        _, b, which = st
                        src = (HN if which == "a" else H)[:, :, b, :]
                        shape = [BLK, NB, HID]
                        if which == "a":
                            read(v, turn, ("gw", 3, 0))
                            read(v, turn, ("gw", 3, 1))
                            v.wait_ge(txt_dma, 32)
                        settle(v.tensor_reduce(st7[:, 0, :], src, AX.X, ALU.add))
                        settle(v.tensor_scalar(st7[:, 0, :], st7[:, 0, :], 1.0 / HID, None, ALU.mult))
                        v.tensor_tensor(XC[:, :, :], src, st7[:, 0, :].unsqueeze(2).to_broadcast(shape),
                                        ALU.subtract).then_inc(centred, 1)
                    elif kind == "ln2":
                        v.wait_ge(squared, nth[st])
                        settle(v.tensor_reduce(st7[:, 1, :], SQ[:, :, :], AX.X, ALU.add))
                        v.tensor_scalar(st7[:, 2, :], st7[:, 1, :], 1.0 / HID, EPS, ALU.mult, ALU.add
                                        ).then_inc(var_ready, 1)
                    elif kind == "ln3":
                        which = st[2]
                        v.wait_ge(rstd_ready, nth[st])
                        twice = [BLK, NB, 2, HID]
                        v.tensor_tensor(XN[which][:, :, :, :], XC[:, :, :].unsqueeze(2).to_broadcast(twice),
                                        st7[:, 3, :].unsqueeze(2).unsqueeze(3).to_broadcast(twice),
                                        ALU.mult).then_inc(normed, 1)
                    elif kind == "xt":
                        v.wait_ge(xt_hi, hi_no[st])
                        tile = XS[st[2]]
                        c0, cn = PIECES[st[3]]
                        v.tensor_tensor(tile[64:128, c0:c0 + cn], T[64:128, 0:cn],
                                        tile[64:128, c0:c0 + cn].bitcast(F32), ALU.subtract).then_inc(free[r], 1)
                    elif kind == "qk":
                        c0, cn = HALVES[st[2]]
                        v.wait_ge(qk_hi, nth[st])
                        v.scalar_tensor_tensor(out=QKL[:, c0:c0 + cn], in0=T[:, 0:cn], scalar=w("b_qk"),
                                               in1=QKH[:, c0:c0 + cn].bitcast(F32), op0=ALU.add, op1=ALU.subtract
                                               ).then_inc(free[r], 1)
                    elif kind == "v":
                        b = st[1]
                        v.wait_ge(full[r], n)
                        v.tensor_tensor(
                            VV[:, b, :, :, 0:HD],
                            T[0:BLK, 0:NB * HID].rearrange("p (k h d) -> p k h d", h=HEADS, d=HD),
                            row("bv").rearrange("p (h d) -> p h d", h=HEADS).unsqueeze(1)
                            .to_broadcast([BLK, NB, HEADS, HD]), ALU.add).then_inc(free[r], 1)
                    elif kind == "ot":
                        _, b, part = st
                        k0, kn = (0, 4) if part == 0 else (4, 3)
                        v.wait_ge(full[r], n)
                        t4 = T[0:BLK, 0:kn * 128].rearrange("p (k h d) -> p k h d", h=HEADS, d=32)
                        settle(v.reciprocal(RC[:, k0:k0 + kn, :], t4[:, :, :, HD]))
                        v.tensor_tensor(OB[:, k0:k0 + kn, :, :], t4[:, :, :, 0:HD],
                                        RC[:, k0:k0 + kn, :].unsqueeze(3).to_broadcast([BLK, kn, HEADS, HD]),
                                        ALU.mult).then_inc(free[r], 1)
                    elif kind == "wo":
                        b = st[1]
                        v.wait_ge(full[r], n)
                        if b == 0:
                            v.wait_ge(hcopied, 1)
                        hb = H[:, :, b, :]
                        ins = v.tensor_tensor(hb, T[0:BLK, 0:NB * HID].rearrange("p (k f) -> p k f", f=HID), hb, ALU.add)
                        ins.then_inc(free[r], 1)
                        v.wait_ge(free[r], n)
                        settle(v.tensor_tensor(hb, hb, row("bo").unsqueeze(1).to_broadcast([BLK, NB, HID]), ALU.add))
                    elif kind == "gate":
                        v.wait_ge(full[r], n)
                        sh = [BLK, NB, EXPERTS]
                        ins = v.tensor_tensor(GZ[:, 0, :, :], T[0:BLK, 0:NB * EXPERTS].rearrange("p (k e) -> p k e", e=EXPERTS),
                                              row("gb", 0, EXPERTS).unsqueeze(1).to_broadcast(sh), ALU.add)
                        ins.then_inc(free[r], 1)
                        v.wait_ge(free[r], n)
                        settle(v.tensor_reduce(GS[:, 0, :], GZ[:, 0, :, :], AX.X, ALU.max))
                        v.tensor_tensor(GZ[:, 0, :, :], GZ[:, 0, :, :], GS[:, 0, :].unsqueeze(2).to_broadcast(sh),
                                        ALU.subtract).then_inc(g_sub, 1)
                    elif kind == "g2":
                        sh = [BLK, NB, EXPERTS]
                        sh4 = [BLK, NB, EXPERTS, EXPERTS]
                        v.wait_ge(g_exp, nth[st])
                        settle(v.tensor_reduce(GS[:, 0, :], GZ[:, 1, :, :], AX.X, ALU.add))
                        settle(v.reciprocal(GS[:, 1, :], GS[:, 0, :]))
                        v.tensor_tensor(GZ[:, 2, :, :], GZ[:, 1, :, :], GS[:, 1, :].unsqueeze(2).to_broadcast(sh),
                                        ALU.mult).then_inc(g_prob, 1)
                        v.wait_ge(g_prob, nth[st])
                        pi = GZ[:, 2, :, :].unsqueeze(3).to_broadcast(sh4)
                        pj = GZ[:, 2, :, :].unsqueeze(2).to_broadcast(sh4)
                        v.tensor_tensor(GC[:, 0, :, :, :], pj, pi, ALU.is_gt)
                        settle(v.tensor_tensor(GC[:, 1, :, :, :], pj, pi, ALU.is_equal))
                        mask = before[0:BLK, :].rearrange("p (i j) -> p i j", i=EXPERTS).unsqueeze(1).to_broadcast(sh4)
                        settle(v.tensor_tensor(GC[:, 1, :, :, :], GC[:, 1, :, :, :], mask, ALU.mult))
                        settle(v.tensor_tensor(GC[:, 0, :, :, :], GC[:, 0, :, :, :], GC[:, 1, :, :, :], ALU.add))
                        settle(v.tensor_reduce(GZ[:, 0, :, :], GC[:, 0, :, :, :], AX.X, ALU.add))
                    elif kind == "g3":
                        sh = [BLK, NB, EXPERTS]
                        v.wait_ge(g_exp2, nth[st])
                        settle(v.scalar_tensor_tensor(out=GZ[:, 1, :, :], in0=GZ[:, 0, :, :], scalar=1.5,
                                                      in1=GZ[:, 3, :, :], op0=ALU.is_lt, op1=ALU.mult))
                        settle(v.tensor_reduce(GS[:, 0, :], GZ[:, 1, :, :], AX.X, ALU.add))
                        settle(v.reciprocal(GS[:, 1, :], GS[:, 0, :]))
                        v.tensor_tensor(GW[:, :, :], GZ[:, 1, :, :], GS[:, 1, :].unsqueeze(2).to_broadcast(sh),
                                        ALU.mult).then_inc(g_weight, 1)
                    elif kind == "wb":
                        _, b, j, t = st
                        c0, cn = PIECES[t]
                        v.wait_ge(full[r], n)
                        read(v, turn, ("l2", b, j, t))
                        v.tensor_tensor(H2[j][:, c0:c0 + cn], T[:, 0:cn], H2[j][:, c0:c0 + cn], ALU.mult
                                        ).then_inc(free[r], 1)
                    elif kind == "back":
                        _, b, t = st
                        image = nth[("l3", b)]
                        k0, kn = (0, 4) if t == 0 else (4, 3)
                        v.wait_ge(full[r], n)
                        v.wait_ge(hb_ready, image)
                        if image > 1:
                            v.wait_ge(out_dma, 16 * (image - 1))
                        v.tensor_tensor(OUTT[:, k0:k0 + kn, :], T[0:BLK, 0:kn * HID].rearrange("p (k f) -> p k f", f=HID),
                                        H[:, k0:k0 + kn, b, :], ALU.add).then_inc(free[r], 1)

            rounds(v, run, report(v))

        @block.tensor
        def _(pe):
            def run(steps, i):
                turn, nth = turns(steps), ordinal(steps)
                if i is None:
                    pe.wait_ge(p_chain, 9)
                for st in steps:
                    kind = st[0]
                    r, n, prior = turn.get(st, (None, 0, ()))
                    if r is not None:
                        T = ps[:, r, :]
                        for rb, nb in prior:
                            pe.wait_ge(free[rb], nb)
                    mm = None
                    if kind == "s":
                        _, b, kb, half, h = st
                        if b == 1 and (kb, half, h) == (0, 0, 0):
                            pe.wait_ge(mrow_dma, 64)
                        c0, cn = HALVES[half]
                        mm = pe.matmul(T[0:BLK, 0:cn], KS[:, b, h, kb * BLK:(kb + 1) * BLK],
                                       QS[:, b, h, c0:c0 + cn], start=True, stop=True)
                    elif kind == "pv":
                        _, b, kb, t = st
                        read(pe, turn, ("s", b, kb, t, HEADS - 1))
                        for h in range(HEADS):
                            pm = pe.matmul(acc[32 * h:32 * h + 32, t, 0:HW], VV[:, b, kb, h, :],
                                           P[:, t, h, :], start=kb == 0, stop=kb == NB - 1,
                                           tile_position=(0, 32 * h))
                        if (kb, t) == (NB - 1, 1):
                            pm.then_inc(full[4], 1)
                        else:
                            pm.then_inc(pv_done, 1)
                    elif kind == "mx":
                        _, b, qb, h, half = st
                        if (qb, h, half) == (0, 0, 0):
                            pe.wait_ge(stack_dma, STACK_LOADS * nth[("stack", b)])
                        c0, cn = HALVES[half]
                        mm = pe.matmul(T[0:BLK, 0:cn], QS[0:SHIFT_ROW, b, h, qb * BLK:(qb + 1) * BLK],
                                       KS[0:SHIFT_ROW, b, h, c0:c0 + cn], start=True, stop=True)
                    elif kind == "mrow":
                        pe.wait_ge(nm_ready, (nth[st] + 1) // 2)
                        for k in range(4) if st[2] == 0 else range(3):
                            qb = k + 4 * st[2]
                            mm = pe.transpose(T[0:HEADS, k * BLK:(k + 1) * BLK],
                                              NMM[:, qb * HEADS:(qb + 1) * HEADS], ident[0:BLK, 0:BLK])
                    elif kind == "embed":
                        half = st[1]
                        pe.wait_ge(x_dma, X_LOADS * (half + 1))
                        for px in range(PATCH):
                            rhs = X[:, :, :].rearrange("p i (j q) -> p i j q", q=PATCH)[:, :, :, px]
                            mm = pe.matmul(T[:, 0:GHALF], w("emb", px, 128)[0:96, :], rhs,
                                           start=px == 0, stop=px == PATCH - 1)
                    elif kind == "gw":
                        _, layer, half = st
                        if half == 0:
                            if layer < 3:
                                pe.wait_ge(ht_scaled, 2 * layer + 2)
                            else:
                                pe.wait_ge(ht_relu, 6)
                        size = GBLK if layer < 3 else BLK
                        rhs = w("gcn", layer, 128) if layer < 3 else w("out")
                        for k in range(4) if half == 0 else range(3):
                            at = (k + 4 * half) * size
                            m = min(size, PATCHES - at)
                            mm = pe.matmul(T[0:m, k * 128:(k + 1) * 128], HT[:, at:at + m], rhs, start=True, stop=True)
                    elif kind == "gagg":
                        _, layer, half = st
                        if half == 0:
                            for g in ("gw", layer, 0), ("gw", layer, 1):
                                read(pe, turn, g)
                        for k in range(NG):
                            for part in (UH, UL):
                                mm = pe.matmul(T[:, 0:GHALF], part[:, k, :], adj[:, k, half * GHALF:(half + 1) * GHALF],
                                               start=k == 0 and part is UH, stop=k == NG - 1 and part is UL)
                    elif kind == "xt":
                        pe.wait_ge(normed, nth[("ln3", st[1], st[2])])
                        for k, at in blocks_of(st[3]):
                            src = XN[st[2]][:, k, :, :].rearrange("p a f -> p (a f)")
                            mm = pe.transpose(T[:, at * BLK:(at + 1) * BLK], src, ident[0:BLK, 0:BLK])
                    elif kind in ("qk", "l1"):
                        b = st[1]
                        which = "a" if kind == "qk" else "m"
                        c0, cn = HALVES[st[-1]]
                        for t in range(2):
                            read(pe, turn, ("xt", b, which, t))
                        name, e, cols = ("qk", 0, 128) if kind == "qk" else \
                            (("eW1", st[2], 128) if st[2] < EXPERTS else ("sW1", 0, 128))
                        for part in (WH, WL):
                            mm = pe.matmul(T[:, 0:cn], wsplit(part, name, e, cols), XS[which][:, c0:c0 + cn],
                                           start=part is WH, stop=part is WL)
                    elif kind in ("v", "gate"):
                        b = st[1]
                        which = "a" if kind == "v" else "m"
                        if kind == "gate" or b == 0:
                            for t in range(2):
                                read(pe, turn, ("xt", b, which, t))
                        cols = HID if kind == "v" else EXPERTS
                        for k in range(NB):
                            for part in (WH, WL):
                                mm = pe.matmul(T[0:BLK, k * cols:(k + 1) * cols], XS[which][:, k * BLK:(k + 1) * BLK],
                                               wsplit(part, "v" if kind == "v" else "gW"),
                                               start=part is WH, stop=part is WL)
                    elif kind == "ot":
                        if st[1] == 0:
                            read(pe, turn, ("pv", 0, 0, 0))
                        for k in range(4) if st[2] == 0 else range(3):
                            at = (k + 4 * st[2]) * BLK
                            mm = pe.transpose(T[0:BLK, k * 128:(k + 1) * 128], OT[:, at:at + BLK], ident[:, :])
                    elif kind == "obt":
                        for part in range(2):
                            read(pe, turn, ("ot", st[1], part))
                        for k in range(NB):
                            mm = pe.transpose(T.bitcast(BF16)[0:64, k * (BLK + 1):k * (BLK + 1) + BLK],
                                              OB[:, k, :, :].rearrange("p h d -> p (h d)"), ident_bf[0:BLK, 0:BLK])
                    elif kind == "wo":
                        read(pe, turn, ("obt", st[1]))
                        for k in range(NB):
                            for part in range(3):
                                mm = pe.matmul(T[0:BLK, k * HID:(k + 1) * HID], OBT[:, k, 0:BLK], wo3[:, part, :],
                                               start=part == 0, stop=part == 2)
                    elif kind == "l2":
                        _, b, j, t = st
                        c0, cn = PIECES[t]
                        experts = (2 * j, 2 * j + 1) if j < 2 else (4,)
                        for e in experts:
                            for half in range(2):
                                read(pe, turn, ("l1", b, e, half))
                        for g, e in enumerate(experts):
                            if j == 2:
                                mm = pe.matmul(T[:, 0:cn], w("sW2"), H1[e % 3][:, c0:c0 + cn], start=True, stop=True)
                            else:
                                mm = pe.matmul(T[64 * g:64 * g + 64, 0:cn], w("eW2", e, 64), H1[e % 3][:, c0:c0 + cn],
                                               start=True, stop=True, tile_position=(0, 64 * g))
                    elif kind == "wb":
                        _, b, j, t = st
                        pe.wait_ge(g_wide, nth[("g3", b)])
                        for k, at in blocks_of(t):
                            src = GWW[:, k, 2 * j:2 * j + 2, :].rearrange("p a f -> p (a f)")
                            mm = pe.transpose(T[:, at * BLK:(at + 1) * BLK], src, ident[0:BLK, 0:BLK])
                    elif kind == "l3":
                        b = st[1]
                        for t in range(2):
                            for s_ in (("wb", b, 0, t), ("wb", b, 1, t), ("l2", b, 2, t)):
                                read(pe, turn, s_)
                        for j in range(3):
                            lhs = w("eW3", j, 64) if j < 2 else w("sW3")
                            for t, (c0, cn) in enumerate(PIECES):
                                mm = pe.matmul(T[64 * t:64 * t + 64, 0:cn], lhs, H2[j][:, c0:c0 + cn],
                                               start=j == 0, stop=j == 2, tile_position=(0, 64 * t))
                    elif kind == "back":
                        read(pe, turn, ("l3", st[1]))
                        t = st[2]
                        for k, at in blocks_of(t):
                            mm = pe.transpose(T[0:BLK, at * HID:(at + 1) * HID],
                                              OT2[64 * t:64 * t + 64, at * BLK:(at + 1) * BLK],
                                              ident[64 * t:64 * t + 64, 64 * t:64 * t + 64])
                    if mm is not None:
                        mm.then_inc(full[r], 1)

            rounds(pe, run, report(pe))


def _stack(*a):
    return np.concatenate(a, axis=0)


def _side(*a):
    return np.concatenate(a, axis=1)


def _diag(m):
    z = np.zeros_like(m)
    return _stack(_side(m, z), _side(z, m))


def _pad(m):
    return _stack(m, np.zeros((128 - m.shape[0], m.shape[1]), m.dtype))


def _twice(m):
    return _stack(m, m)


def _col(b):
    return np.reshape(b, (-1, 1))


def constants():
    ident = np.eye(128, dtype=np.float32)
    pos = np.arange(PATCHES, dtype=np.float32)[:, None]
    div = np.exp(np.arange(0, HID, 2, dtype=np.float32) * np.float32(-np.log(10000.0) / HID)).astype(np.float32)
    pe = np.zeros((PATCHES, HID), np.float32)
    pe[:, 0::2] = np.sin(pos * div)
    pe[:, 1::2] = np.cos(pos * div)
    iota = np.broadcast_to(np.arange(PATCHES, dtype=np.float32), (128, PATCHES))
    before = np.tril(np.ones((EXPERTS, EXPERTS), np.float32), -1).reshape(1, -1)
    return np.ascontiguousarray(_side(ident, _twice(pe.T), iota, np.broadcast_to(before, (128, 16))))


def layout(i):
    i = {k: np.asarray(v) for k, v in i.items()}
    t, a, f = "L0_tok_", "L0_attn_", "L0_ffn_"
    we = i[t + "W_embed"].reshape(CH * PATCH, PATCH, HID)
    emb = _side(*[_pad(_diag(we[:, px, :])) for px in range(PATCH)])
    gcn = _side(*[_diag(i[t + "W_gcn"][n]) for n in range(3)])
    plain = _side(emb, gcn, _diag(i[t + "W_out"]), _pad(i[a + "Wo"].T),
                  *[i[f + "eW2"][e] for e in range(EXPERTS)], _pad(i[f + "sW2"]),
                  _stack(i[f + "eW3"][0], i[f + "eW3"][1]), _stack(i[f + "eW3"][2], i[f + "eW3"][3]), i[f + "sW3"],
                  _col(_twice(i[t + "b_embed"])), *[_col(_twice(i[t + "b_gcn"][n])) for n in range(3)],
                  _col(_stack(i[a + "bq"], i[a + "bk"])), *[_col(i[f + "eb1"][e]) for e in range(EXPERTS)],
                  _col(_twice(i[f + "sb1"])), _col(_stack(i[f + "eb2"][0], i[f + "eb2"][1])),
                  _col(_stack(i[f + "eb2"][2], i[f + "eb2"][3])), _col(i[f + "sb2"]))
    split = _twice(_side(i[a + "Wq"].T, i[a + "Wk"].T, i[a + "Wv"].T, *[i[f + "eW1"][e] for e in range(EXPERTS)],
                         i[f + "sW1"], i[f + "sW1"], i[f + "gW"]))
    rows = np.concatenate([i[t + "b_out"], i[a + "bv"], i[a + "bo"], i[f + "gb"], i[f + "sb3"],
                           i[f + "eb3"].reshape(-1)]).reshape(1, -1)
    return {"x": i["x"], "txt": i["txt"], "edges": i[t + "edge_index"], "plain": plain, "split": split,
            "rows": rows, "const": constants()}


def kernel(**inputs):
    import concourse.bacc as bacc
    from concourse.bass_utils import run_bass_kernel_spmd

    nc = bacc.Bacc("TRN2", target_bir_lowering=False, num_devices=1)
    arrays = {f"in_{k}": np.ascontiguousarray(v) for k, v in layout(inputs).items()}
    args = [nc.dram_tensor(k, v.shape, mybir.dt.from_np(v.dtype), kind="ExternalInput").ap() for k, v in arrays.items()]
    batch = arrays["in_x"].shape[0]
    out = nc.dram_tensor("out_0", (batch, TOKENS, HID), F32, kind="ExternalOutput").ap()
    build(nc, batch // 2, *args, out)
    r = run_bass_kernel_spmd(nc, [arrays], core_ids=[0])
    return r.results[0]["out_0"]
```
